# Optimizing a Trainium2 kernel written in Bass

```python
import numpy as np
import jax
import jax.numpy as jnp

def _softmax(x, axis=-1):
    return jax.nn.softmax(x, axis=axis)

def _gelu(x):
    return jax.nn.gelu(x, approximate=True)

def _silu(x):
    return jax.nn.silu(x)

def _sigmoid(x):
    return jax.nn.sigmoid(x)

def _layernorm(x, axis=-1, eps=1e-05):
    m = jnp.mean(x, axis=axis, keepdims=True)
    v = jnp.var(x, axis=axis, keepdims=True)
    return (x - m) / jnp.sqrt(v + eps)

def _scatter_add(tgt, idx, src, axis=0):
    return tgt.at[idx].add(src)

def _segment_sum(src, seg, n):
    return jax.ops.segment_sum(src, seg, n)
kernel_name = 'mk_decoder_postln_d1_seqx_r8_41d2c4'

def setup_inputs(seed: int=0):
    np.random.seed(seed)
    _w = jnp.asarray

    def _rec_inputs():
        import jax
        import jax.numpy as jnp
        _rk = jax.random.key(seed)
        x = -0.000125 + 0.9999 * jax.random.normal(jax.random.fold_in(_rk, 1), (32, 64, 512), jnp.float32)
        _lenS = 64 - jax.random.randint(jax.random.fold_in(_rk, 7), (32,), 0, max(1, 64 // 4) + 1, jnp.int32)
        _lenS2 = 64 - jax.random.randint(jax.random.fold_in(_rk, 8), (32,), 0, max(1, 64 // 4) + 1, jnp.int32)
        _ctx_4096P = jax.random.normal(jax.random.fold_in(_rk, 11), (32, 16, 512), jnp.float32)
        _ctx_4096c = jax.random.dirichlet(jax.random.fold_in(_rk, 511), 0.3 * jnp.ones((16,), jnp.float32), (32, 64))
        _ctx_4096t = jnp.einsum('bsk,bkd->bsd', _ctx_4096c, _ctx_4096P)
        _ctx_4096t = _ctx_4096t * jax.lax.rsqrt(jnp.mean(jnp.square(_ctx_4096t)) + 1e-12) * 0.953939
        ctx_4096 = -1.52775e-05 + 0.999936 * (_ctx_4096t + 0.3 * jax.random.normal(jax.random.fold_in(_rk, 611), (32, 64, 512), jnp.float32))
        return (x, ctx_4096)
    x, ctx_4096 = _rec_inputs()

    def _L0_attn_setup():
        import jax, jax.numpy as jnp
        import numpy as np
        NUM_Q_HEADS = 32
        NUM_KV_GROUPS = 8
        HEAD_SIZE = 128
        ROPE_THETA = 10000.0

        def _rope_cos_sin(T, dim, dtype=jnp.float32):
            freqs = 1.0 / ROPE_THETA ** (jnp.arange(0, dim, 2, dtype=jnp.float32) / dim)
            angle = jnp.arange(T, dtype=jnp.float32)[:, None] * freqs[None, :]
            return (jnp.cos(angle).astype(dtype), jnp.sin(angle).astype(dtype))

        def _apply_rope(x, cos, sin):
            xr = x[..., 0::2]
            xi = x[..., 1::2]
            or_ = xr * cos - xi * sin
            oi_ = xr * sin + xi * cos
            out = jnp.stack([or_, oi_], axis=-1)
            return out.reshape(x.shape)
        key = jax.random.key(seed)
        ks = jax.random.split(key, 5)
        B, T, C = (2, 128, 512)
        H, G, D = (NUM_Q_HEADS, NUM_KV_GROUPS, HEAD_SIZE)
        s = 1.0 / np.sqrt(C)
        return {'x': jax.random.normal(ks[0], (B, T, C), dtype=jnp.float32), 'Wq': jax.random.normal(ks[1], (C, H * D), dtype=jnp.float32) * s, 'Wk': jax.random.normal(ks[2], (C, G * D), dtype=jnp.float32) * s, 'Wv': jax.random.normal(ks[3], (C, G * D), dtype=jnp.float32) * s, 'Wo': jax.random.normal(ks[4], (H * D, C), dtype=jnp.float32) * (1.0 / np.sqrt(H * D)), 'bo': jnp.zeros((C,), dtype=jnp.float32)}
    _L0_attn_all = _L0_attn_setup()
    _L0_attn_in = {k: v for k, v in _L0_attn_all.items() if k in ('Wq', 'Wk', 'Wv', 'Wo', 'bo')}
    del _L0_attn_all

    def _L0_xattn_setup():
        import jax, jax.numpy as jnp
        import numpy as np
        NUM_HEADS = 8

        def _proj(W, b, x):
            return jnp.einsum('oi,bil->bol', W, x) + b[:, None]
        key = jax.random.key(seed)
        ks = jax.random.split(key, 11)
        B, D, L = (16, 64, 512)
        s = 1.0 / np.sqrt(D).astype(np.float32)
        return {'x_query': jax.random.normal(ks[0], (B, D, L), jnp.float32), 'x_key': jax.random.normal(ks[1], (B, D, L), jnp.float32), 'x_value': jax.random.normal(ks[2], (B, D, L), jnp.float32), 'Wq': jax.random.normal(ks[3], (D, D), jnp.float32) * s, 'bq': jax.random.normal(ks[4], (D,), jnp.float32) * 0.01, 'Wk': jax.random.normal(ks[5], (D, D), jnp.float32) * s, 'bk': jax.random.normal(ks[6], (D,), jnp.float32) * 0.01, 'Wv': jax.random.normal(ks[7], (D, D), jnp.float32) * s, 'bv': jax.random.normal(ks[8], (D,), jnp.float32) * 0.01, 'Wo': jax.random.normal(ks[9], (D, D), jnp.float32) * s, 'bo': jax.random.normal(ks[10], (D,), jnp.float32) * 0.01}
    _L0_xattn_all = _L0_xattn_setup()
    _L0_xattn_in = {k: v for k, v in _L0_xattn_all.items() if k in ('Wq', 'bq', 'Wk', 'bk', 'Wv', 'bv', 'Wo', 'bo')}
    del _L0_xattn_all

    def _L0_ffn_setup():
        import jax, jax.numpy as jnp
        import numpy as np

        @jax.custom_vjp
        def ste_sign(w):
            return jnp.sign(w)

        def _ste_fwd(w):
            return (jnp.sign(w), w)

        def _ste_bwd(w, g):
            mask = ((w > -1) & (w < 1)).astype(g.dtype)
            return (g * mask,)
        ste_sign.defvjp(_ste_fwd, _ste_bwd)
        key = jax.random.key(seed)
        k = jax.random.split(key, 6)
        B, S, H, O, E = (4, 256, 512, 512, 8)
        return {'x': jax.random.normal(k[0], (B, S, H), dtype=jnp.float32), 'weight': jax.random.normal(k[1], (O, H), dtype=jnp.float32) * 0.02, 'bias': jax.random.normal(k[2], (O,), dtype=jnp.float32) * 0.02, 'gate_w': jax.random.normal(k[3], (E, H), dtype=jnp.float32) * 0.02, 'in_channel_scale': jax.random.normal(k[4], (E, H), dtype=jnp.float32), 'out_channel_scale': jax.random.normal(k[5], (E, O), dtype=jnp.float32)}
    _L0_ffn_all = _L0_ffn_setup()
    _L0_ffn_in = {k: v for k, v in _L0_ffn_all.items() if k in ('weight', 'bias', 'gate_w', 'in_channel_scale', 'out_channel_scale')}
    del _L0_ffn_all
    return {'x': x, 'ctx_4096': ctx_4096, 'L0_attn_Wq': _L0_attn_in['Wq'], 'L0_attn_Wk': _L0_attn_in['Wk'], 'L0_attn_Wv': _L0_attn_in['Wv'], 'L0_attn_Wo': _L0_attn_in['Wo'], 'L0_attn_bo': _L0_attn_in['bo'], 'L0_xattn_Wq': _L0_xattn_in['Wq'], 'L0_xattn_bq': _L0_xattn_in['bq'], 'L0_xattn_Wk': _L0_xattn_in['Wk'], 'L0_xattn_bk': _L0_xattn_in['bk'], 'L0_xattn_Wv': _L0_xattn_in['Wv'], 'L0_xattn_bv': _L0_xattn_in['bv'], 'L0_xattn_Wo': _L0_xattn_in['Wo'], 'L0_xattn_bo': _L0_xattn_in['bo'], 'L0_ffn_weight': _L0_ffn_in['weight'], 'L0_ffn_bias': _L0_ffn_in['bias'], 'L0_ffn_gate_w': _L0_ffn_in['gate_w'], 'L0_ffn_in_channel_scale': _L0_ffn_in['in_channel_scale'], 'L0_ffn_out_channel_scale': _L0_ffn_in['out_channel_scale']}

def reference(x, ctx_4096, L0_attn_Wq, L0_attn_Wk, L0_attn_Wv, L0_attn_Wo, L0_attn_bo, L0_xattn_Wq, L0_xattn_bq, L0_xattn_Wk, L0_xattn_bk, L0_xattn_Wv, L0_xattn_bv, L0_xattn_Wo, L0_xattn_bo, L0_ffn_weight, L0_ffn_bias, L0_ffn_gate_w, L0_ffn_in_channel_scale, L0_ffn_out_channel_scale):
    import jax
    import jax.numpy as jnp

    def _L0_attn_ref(x, Wq, Wk, Wv, Wo, bo):
        import jax, jax.numpy as jnp
        import numpy as np
        NUM_Q_HEADS = 32
        NUM_KV_GROUPS = 8
        HEAD_SIZE = 128
        ROPE_THETA = 10000.0

        def _rope_cos_sin(T, dim, dtype=jnp.float32):
            freqs = 1.0 / ROPE_THETA ** (jnp.arange(0, dim, 2, dtype=jnp.float32) / dim)
            angle = jnp.arange(T, dtype=jnp.float32)[:, None] * freqs[None, :]
            return (jnp.cos(angle).astype(dtype), jnp.sin(angle).astype(dtype))

        def _apply_rope(x, cos, sin):
            xr = x[..., 0::2]
            xi = x[..., 1::2]
            or_ = xr * cos - xi * sin
            oi_ = xr * sin + xi * cos
            out = jnp.stack([or_, oi_], axis=-1)
            return out.reshape(x.shape)
        B, T, C = x.shape
        H, G, D = (NUM_Q_HEADS, NUM_KV_GROUPS, HEAD_SIZE)
        rep = H // G
        q = (x @ Wq).reshape(B, T, H, D).transpose(0, 2, 1, 3)
        k = (x @ Wk).reshape(B, T, G, D).transpose(0, 2, 1, 3)
        v = (x @ Wv).reshape(B, T, G, D).transpose(0, 2, 1, 3)
        cos, sin = _rope_cos_sin(T, D)
        q = _apply_rope(q, cos, sin)
        k = _apply_rope(k, cos, sin)
        qg = q.reshape(B, G, rep, T, D)
        scores = jnp.einsum('bgrtd,bgsd->bgrts', qg, k) * D ** (-0.5)
        causal = jnp.tril(jnp.ones((T, T), dtype=bool))
        scores = jnp.where(causal, scores, -jnp.inf)
        probs = jax.nn.softmax(scores, axis=-1)
        out = jnp.einsum('bgrts,bgsd->bgrtd', probs, v)
        out = out.reshape(B, H, T, D).transpose(0, 2, 1, 3).reshape(B, T, H * D)
        return out @ Wo + bo

    def _L0_xattn_ref(x_query, x_key, x_value, Wq, bq, Wk, bk, Wv, bv, Wo, bo):
        import jax, jax.numpy as jnp
        import numpy as np
        NUM_HEADS = 8

        def _proj(W, b, x):
            return jnp.einsum('oi,bil->bol', W, x) + b[:, None]
        B, D, L = x_query.shape
        h = NUM_HEADS
        Lh = L // h
        q = _proj(Wq, bq, x_query)
        k = _proj(Wk, bk, x_key)
        v = _proj(Wv, bv, x_value)
        qh = q.reshape(B, D, h, Lh).transpose(2, 0, 1, 3)
        kh = k.reshape(B, D, h, Lh).transpose(2, 0, 1, 3)
        vh = v.reshape(B, D, h, Lh).transpose(2, 0, 1, 3)
        scale = 1.0 / jnp.sqrt(jnp.asarray(Lh, x_query.dtype))
        scores = jnp.einsum('hbdk,hbek->hbde', qh, kh) * scale
        p = jax.nn.softmax(scores, axis=-1)
        xh = jnp.einsum('hbde,hbek->hbdk', p, vh)
        x = xh.transpose(1, 2, 0, 3).reshape(B, D, L)
        return _proj(Wo, bo, x)

    def _L0_ffn_ref(x, weight, bias, gate_w, in_channel_scale, out_channel_scale):
        import jax, jax.numpy as jnp
        import numpy as np

        @jax.custom_vjp
        def ste_sign(w):
            return jnp.sign(w)

        def _ste_fwd(w):
            return (jnp.sign(w), w)

        def _ste_bwd(w, g):
            mask = ((w > -1) & (w < 1)).astype(g.dtype)
            return (g * mask,)
        ste_sign.defvjp(_ste_fwd, _ste_bwd)
        B, S, H = x.shape
        xf = x.reshape(-1, H)
        router_logits = xf @ gate_w.T
        routing = jax.nn.softmax(router_logits.astype(jnp.float32), axis=1).astype(x.dtype)
        in_scale = routing @ in_channel_scale
        out_scale = routing @ out_channel_scale
        wb = ste_sign(weight)
        out = xf * in_scale @ wb.T * out_scale + bias
        return out.reshape(B, S, -1)
    x = _layernorm(x + _L0_attn_ref(x, L0_attn_Wq, L0_attn_Wk, L0_attn_Wv, L0_attn_Wo, L0_attn_bo), axis=-1)
    x = _layernorm(x + _L0_xattn_ref(x, ctx_4096, ctx_4096, L0_xattn_Wq, L0_xattn_bq, L0_xattn_Wk, L0_xattn_bk, L0_xattn_Wv, L0_xattn_bv, L0_xattn_Wo, L0_xattn_bo), axis=-1)
    x = _layernorm(x + _L0_ffn_ref(x, L0_ffn_weight, L0_ffn_bias, L0_ffn_gate_w, L0_ffn_in_channel_scale, L0_ffn_out_channel_scale), axis=-1)
    return x

_drawn_inputs = setup_inputs


def setup_inputs(seed=0):
    import zlib

    import numpy as np

    out = dict(_drawn_inputs(seed))
    spreads = {'L0_attn_bo': (0.0, 0.1)}
    factors = {'L0_xattn_bq': 23.243,
     'L0_xattn_bk': 21.416,
     'L0_xattn_bv': 43.519,
     'L0_xattn_bo': 64.0,
     'L0_ffn_bias': 8.0}
    for name, (base, spread) in spreads.items():
        noise = np.random.default_rng([zlib.crc32(name.encode()), seed]).standard_normal(out[name].shape)
        drawn = base * np.exp(spread * noise) if base else spread * noise
        out[name] = jnp.asarray(drawn.astype(out[name].dtype))
    for name, factor in factors.items():
        out[name] = (out[name] * factor).astype(out[name].dtype)
    return out
```

```python
from contextlib import ExitStack

import concourse.bass as bass
import numpy as np
from concourse import mybir

ALU = mybir.AluOpType
ACT = mybir.ActivationFunctionType
AX_X = mybir.AxisListType.X
F32 = mybir.dt.float32
F32R = mybir.dt.float32r

P = 128
BANK = 512
B, T, C = 32, 64, 512
TOKENS = B * T
G, REP, D = 8, 4, 128
KT = C // P
CHUNK = 512
CHUNKS = TOKENS // CHUNK
PAIRS = CHUNK // P
TILES = TOKENS // P
GCOLS = (REP + 2) * D
XH, LH = 8, 64
E = 8
EPS = 1e-5
ATTN_SCALE = float(D) ** -0.5
CROSS_SCALE = float(LH) ** -0.5
MASKED = -1e38
PROJ_TILES = REP + 2
ROPE_TILES = REP + 1
COS, SIN, MASK, IDENT, CONSTS = 0, T, 2 * T, 3 * T, 3 * T + P
BANK_PROJ, BANK_SCORE, BANK_TURN, BANK_ACC = 0, 2, 4, 6


def decoder_layer(nc, x, ctx, wqkv, wo, attn_bo, consts, x_wq, x_bq, x_wk, x_bk, x_wv, x_bv,
                  x_wo, x_bo, f_w, f_bias, f_gate, f_in, f_out, out):
    outer = ExitStack()
    with outer:
        def sem(name):
            return outer.enter_context(nc.semaphore(name))

        def sb(stack, name, shape, dt=F32):
            return stack.enter_context(nc.sbuf_tensor(name, shape, dt))

        ps = outer.enter_context(nc.psum_tensor("ps", [P, 8, BANK], F32))
        resid = sb(outer, "resid", [P, TILES, C])
        const = sb(outer, "const", [P, CONSTS])
        cos, sin = const[:, COS:COS + T], const[:, SIN:SIN + T]
        causal, ident = const[:, MASK:MASK + T], const[:, IDENT:IDENT + P]

        one = ExitStack()
        x_high = sb(one, "x_high", [P, KT, TOKENS], F32R)
        x_low = sb(one, "x_low", [P, KT, TOKENS], F32R)
        w_high = sb(one, "w_high", [P, KT, GCOLS], F32R)
        w_low = sb(one, "w_low", [P, KT, GCOLS], F32R)
        wo_high = sb(one, "wo_high", [P, REP, C], F32R)
        wo_low = sb(one, "wo_low", [P, REP, C], F32R)
        stage = sb(one, "stage", [P, KT, GCOLS])
        q_rot = sb(one, "q_rot", [P, 2, 8, 2, T])
        k_rot = sb(one, "k_rot", [P, CHUNK])
        by_cos = sb(one, "by_cos", [P, 2, CHUNK])
        swapped = sb(one, "swapped", [P, 2, CHUNK])
        prob = sb(one, "prob", [P, 16, T])
        pt_high = sb(one, "pt_high", [P, PAIRS, 2, 2 * P], F32R)
        pt_low = sb(one, "pt_low", [P, PAIRS, 2, 2 * P], F32R)
        v_turn = sb(one, "v_turn", [P, CHUNK])
        v_high = sb(one, "v_high", [P, PAIRS, D], F32R)
        v_low = sb(one, "v_low", [P, PAIRS, D], F32R)
        o_high = sb(one, "o_high", [P, 2, REP, P], F32R)
        o_low = sb(one, "o_low", [P, 2, REP, P], F32R)
        row_max = sb(one, "row_max", [P, 16])
        row_sum = sb(one, "row_sum", [P, 16])
        row_inv = sb(one, "row_inv", [P, 16])
        bo_row = prob[:, 0:8, :].rearrange("p a b -> p (a b)")
        stage_wo = stage[:, :, :].rearrange("p a b -> p (a b)")[:, 0:REP * C].rearrange("p (a b) -> p a b", a=REP)
        one.close()

        two = outer
        ctx_t = sb(two, "ctx_t", [P, 2, C])
        x1 = sb(two, "x1", [P, 2, C])
        x2 = sb(two, "x2", [P, 2, C])
        x2_biased = sb(two, "x2_biased", [P, 2, C])
        x2_turn = sb(two, "x2_turn", [P, 2, KT, P])
        xq_turn = sb(two, "xq_turn", [P, KT, P])
        xk_turn = sb(two, "xk_turn", [P, KT, P])
        xv = sb(two, "xv", [P, 2, C])
        xprob = sb(two, "xprob", [P, XH, LH])
        xdiag = sb(two, "xdiag", [P, XH, P])
        xdiag_turn = sb(two, "xdiag_turn", [P, XH, P])
        xmix = sb(two, "xmix", [P, C])
        xsum2 = sb(two, "xsum2", [P, C])
        u = sb(two, "u", [P, KT, P])
        u_high = sb(two, "u_high", [P, KT, P], F32R)
        u_low = sb(two, "u_low", [P, KT, P], F32R)
        out_scale = sb(two, "out_scale", [P, C])
        xsum3 = sb(two, "xsum3", [P, C])
        final = sb(two, "final", [P, 2, C])
        sign_w = sb(two, "sign_w", [P, KT, C], F32R)
        raw_w = sb(two, "raw_w", [P, KT, C])
        below = sb(two, "below", [P, C])
        fbias_row = sb(two, "fbias_row", [P, C])
        blocks = sb(two, "blocks", [P, 4, P])
        bias_rows = sb(two, "bias_rows", [P, 2, P])
        bias_cols = sb(two, "bias_cols", [P, 2])
        gate_w = sb(two, "gate_w", [P, KT, E])
        in_cs = sb(two, "in_cs", [E, C])
        out_cs = sb(two, "out_cs", [E, C])
        stats = sb(two, "stats", [P, 3, 6])
        moments = sb(two, "moments", [P, 3, 2])
        var_eps = sb(two, "var_eps", [P, 3])
        rstd = sb(two, "rstd", [P, 3])
        minus_half = sb(two, "minus_half", [P, 1])
        x_max = sb(two, "x_max", [P, XH])
        x_sum = sb(two, "x_sum", [P, XH])
        x_inv = sb(two, "x_inv", [P, XH])
        r_max = sb(two, "r_max", [P, 1])
        r_exp = sb(two, "r_exp", [P, E])
        r_sum = sb(two, "r_sum", [P, 1])
        r_inv = sb(two, "r_inv", [P, 1])
        routing = sb(two, "routing", [P, E])
        routing_turn = sb(two, "routing_turn", [E, P])

        x_loaded = [sem(f"x_loaded{c}") for c in range(CHUNKS)]
        const_loaded = sem("const_loaded")
        wqkv_loaded, wo_loaded = sem("wqkv_loaded"), sem("wo_loaded")
        x_turned, x_high_done, x_low_done = sem("x_turned"), sem("x_high_done"), sem("x_low_done")
        zeroed, biased = sem("zeroed"), sem("biased")
        w_high_done, w_low_done = sem("w_high_done"), sem("w_low_done")
        wo_high_done, wo_low_done = sem("wo_high_done"), sem("wo_low_done")
        projected = sem("projected")
        swap_done, cos_done, sin_done, rotated = sem("swap_done"), sem("cos_done"), sem("sin_done"), sem("rotated")
        scored, masked, max_done, shifted = sem("scored"), sem("masked"), sem("max_done"), sem("shifted")
        exp_done, sum_done, inv_done, normed = sem("exp_done"), sem("sum_done"), sem("inv_done"), sem("normed")
        pt_turned, pt_high_done, pt_low_done = sem("pt_turned"), sem("pt_high_done"), sem("pt_low_done")
        v_copied, v_turned, v_high_done, v_low_done = (
            sem("v_copied"), sem("v_turned"), sem("v_high_done"), sem("v_low_done"))
        mixed, o_high_done, o_low_done = sem("mixed"), sem("o_high_done"), sem("o_low_done")
        out_projected, resid_added = sem("out_projected"), sem("resid_added")

        small_loaded, blocks_loaded = sem("small_loaded"), sem("blocks_loaded")
        ctx_loaded = [sem("ctx_loaded0"), sem("ctx_loaded1")]
        blocks_zeroed, diag_zeroed = sem("blocks_zeroed"), sem("diag_zeroed")
        sign_step = sem("sign_step")
        norm_step = [sem(f"norm_step{k}") for k in (1, 2, 3)]
        rstd_done = [sem(f"rstd_done{k}") for k in (1, 2, 3)]
        x1_done, x2_done, x3_done = sem("x1_done"), sem("x2_done"), sem("x3_done")
        k_projected, v_projected, q_projected = sem("k_projected"), sem("v_projected"), sem("q_projected")
        k_copied, xv_copied, q_copied = sem("k_copied"), sem("xv_copied"), sem("q_copied")
        x_scored, x_max_done, x_shifted, x_exp_done = (
            sem("x_scored"), sem("x_max_done"), sem("x_shifted"), sem("x_exp_done"))
        x_sum_done, x_inv_done, x_normed = sem("x_sum_done"), sem("x_inv_done"), sem("x_normed")
        diag_turned, diag_copied = sem("diag_turned"), sem("diag_copied")
        x_mixed, mix_copied, cross_done, sum2_done = (
            sem("x_mixed"), sem("mix_copied"), sem("cross_done"), sem("sum2_done"))
        x2_biased_done, x2_turned, x2_copied = sem("x2_biased_done"), sem("x2_turned"), sem("x2_copied")
        logits_done, r_max_done, r_exp_done, r_inv_done, routed = (
            sem("logits_done"), sem("r_max_done"), sem("r_exp_done"), sem("r_inv_done"), sem("routed"))
        routing_turned, routing_copied = sem("routing_turned"), sem("routing_copied")
        in_scaled, u_done, u_high_done, u_low_done = (
            sem("in_scaled"), sem("u_done"), sem("u_high_done"), sem("u_low_done"))
        out_scale_ready, out_scale_copied = sem("out_scale_ready"), sem("out_scale_copied")
        signed_done, scaled_done, sum3_done, stored = (
            sem("signed_done"), sem("scaled_done"), sem("sum3_done"), [sem("stored0"), sem("stored1")])

        block = outer.enter_context(nc.Block())
        ALL = G * CHUNKS

        def over_groups(eng, iteration, finish):
            for c in range(CHUNKS):
                iteration(c, 0, c, c == 0, False)
            with eng.Fori(1, G - 1) as g:
                for c in range(CHUNKS):
                    iteration(g * CHUNKS + c, g, c, False, False)
            for c in range(CHUNKS):
                iteration(ALL - CHUNKS + c, G - 1, c, False, True)
            finish(ALL)

        PEEL, TAIL = 6, 3

        def over_tiles(eng, step):
            for i in range(PEEL):
                step(i, i % 2, True, i >= 1, i >= 2, i >= 3)
            with eng.Fori(0, (TILES - PEEL) // 2) as h:
                for odd in range(2):
                    step(h * 2 + (PEEL + odd), odd, True, True, True, True)
            for i in range(TILES, TILES + TAIL):
                step(i, i % 2, False, i < TILES + 1, i < TILES + 2, True)

        def score_columns(b, j):
            return (b // 2) * 4 + 2 * j + b % 2

        @block.sync
        def _(sp):
            sp.dma_start(const[:, :], consts).then_inc(const_loaded, 16)
            xt = x.rearrange("(i p) c -> p i c", p=P)
            for c in range(CHUNKS):
                sp.dma_start(resid[:, c * PAIRS:(c + 1) * PAIRS, :],
                             xt[:, c * PAIRS:(c + 1) * PAIRS, :]).then_inc(x_loaded[c], 16)
                if c == 0:
                    sp.dma_start(stage[:, :, :], wqkv[0]).then_inc(wqkv_loaded, 16)
                    sp.dma_start(bo_row, attn_bo.partition_broadcast(P)).then_inc(const_loaded, 16)

            def load_wo(g):
                sp.wait_ge(w_low_done, g + 1)
                sp.dma_start(stage_wo, wo[g]).then_inc(wo_loaded, 16)

            def load_wqkv(g):
                sp.wait_ge(wo_low_done, g)
                sp.dma_start(stage[:, :, :], wqkv[g]).then_inc(wqkv_loaded, 16)

            load_wo(0)
            with sp.Fori(1, G) as g:
                load_wqkv(g)
                load_wo(g)

            sp.wait_ge(projected, ALL * PROJ_TILES)
            sp.dma_start(raw_w[:, :, :], f_w.rearrange("(k p) o -> p k o", p=P)).then_inc(small_loaded, 16)
            sp.dma_start(fbias_row[:, :], f_bias.partition_broadcast(P)).then_inc(small_loaded, 16)
            sp.dma_start(gate_w[:, :, :], f_gate.rearrange("(k p) e -> p k e", p=P)).then_inc(small_loaded, 16)
            sp.dma_start(in_cs[:, :], f_in).then_inc(small_loaded, 16)
            sp.dma_start(out_cs[:, :], f_out).then_inc(small_loaded, 16)
            for k, bias in enumerate((x_bq, x_bk)):
                for b in range(2):
                    sp.dma_start(bias_rows[:, k, b * T:(b + 1) * T],
                                 bias.partition_broadcast(P)).then_inc(small_loaded, 16)
            for k, bias in enumerate((x_bv, x_bo)):
                for b in range(2):
                    sp.dma_start(bias_cols[b * T:(b + 1) * T, k:k + 1],
                                 bias.rearrange("(p o) -> p o", o=1)).then_inc(small_loaded, 16)
            SMALL = 16 * 13
            sp.wait_ge(blocks_zeroed, 1)
            for k, w in enumerate((x_wq, x_wk, x_wv, x_wo)):
                for b in range(2):
                    sp.dma_start(blocks[b * T:(b + 1) * T, k, b * T:(b + 1) * T], w).then_inc(blocks_loaded, 16)

            ct = ctx.rearrange("(i p) c -> i p c", p=P)
            ot = out.rearrange("(i p) c -> i p c", p=P)

            def step(i, odd, a, b, c, d):
                if a:
                    if not isinstance(i, int) or i >= 2:
                        sp.wait_ge(v_projected, i - 1)
                    sp.dma_start(ctx_t[:, odd, :], ct[i] if isinstance(i, int) else
                                 ctx[bass.ts(i, P), :]).then_inc(ctx_loaded[odd], 16)
                if d:
                    t = i - 3
                    sp.wait_ge(x3_done, t + 1)
                    sp.dma_start(ot[t] if isinstance(t, int) else out[bass.ts(t, P), :],
                                 final[:, 1 - odd, :]).then_inc(stored[1 - odd], 16)

            over_tiles(sp, step)
            for s in stored:
                sp.wait_ge(s, 16 * TILES // 2)

        @block.tensor
        def _(pe):
            mm = nc.tensor.matmul
            pe.wait_ge(const_loaded, 32)
            for t in range(TILES):
                if t % PAIRS == 0:
                    pe.wait_ge(x_loaded[t // PAIRS], 16)
                if t >= 8:
                    pe.wait_ge(x_low_done, t - 7)
                for k in range(KT):
                    last = nc.tensor.transpose(ps[:, t % 8, k * P:(k + 1) * P],
                                               resid[:, t, k * P:(k + 1) * P], ident)
                last.then_inc(x_turned, 1)
            pe.wait_ge(x_low_done, TILES)

            def project(j, c):
                acc = ps[:, BANK_PROJ + j % 2, :]
                cols = slice(j * D, (j + 1) * D)
                tok = slice(c * CHUNK, (c + 1) * CHUNK)
                for k in range(KT):
                    mm(acc, w_high[:, k, cols], x_high[:, k, tok], start=(k == 0), stop=False)
                    mm(acc, w_high[:, k, cols], x_low[:, k, tok], start=False, stop=False)
                    last = mm(acc, w_low[:, k, cols], x_high[:, k, tok], start=False, stop=(k == KT - 1))
                last.then_inc(projected, 1)

            def turn_probs(m):
                for h in range(2):
                    pe.wait_ge(normed, 2 * m + h + 1)
                    for q in range(2):
                        for j in range(2):
                            seg = (2 * h + q) * 4 + 2 * j
                            last = nc.tensor.transpose(
                                ps[:, BANK_TURN + h, (2 * q + j) * P:(2 * q + j + 1) * P],
                                prob[:, seg:seg + 2, :].rearrange("p a b -> p (a b)"), ident)
                    last.then_inc(pt_turned, 1)

            def mix(m, r):
                bank = (BANK_ACC, BANK_ACC + 1, BANK_TURN, BANK_TURN + 1)[r]
                pe.wait_ge(pt_low_done, 2 * m + r // 2 + 1)
                pe.wait_ge(v_low_done, m + 1)
                if r == 2:
                    pe.wait_ge(pt_low_done, 2 * m + 1)
                rhs_high = pt_high[:, r, :, :].rearrange("p a b -> p (a b)")
                rhs_low = pt_low[:, r, :, :].rearrange("p a b -> p (a b)")
                mm(ps[:, bank, :], v_high[:, r, :], rhs_high, start=True, stop=False)
                mm(ps[:, bank, :], v_high[:, r, :], rhs_low, start=False, stop=False)
                mm(ps[:, bank, :], v_low[:, r, :], rhs_high, start=False, stop=True).then_inc(mixed, 1)

            def out_project(m, r):
                pe.wait_ge(o_low_done, 4 * m + r + 1)
                if r >= 2:
                    pe.wait_ge(resid_added, 4 * m + r - 1)
                acc = ps[:, BANK_ACC + r % 2, :]
                for h in range(REP):
                    mm(acc, o_high[:, r % 2, h, :], wo_high[:, h, :], start=(h == 0), stop=False)
                    mm(acc, o_high[:, r % 2, h, :], wo_low[:, h, :], start=False, stop=False)
                    last = mm(acc, o_low[:, r % 2, h, :], wo_high[:, h, :], start=False, stop=(h == REP - 1))
                last.then_inc(out_projected, 1)

            def attention_a(m):
                if not isinstance(m, int) or m >= 1:
                    pe.wait_ge(o_low_done, 4 * m)
                turn_probs(m)

            def attention_b(m):
                if not isinstance(m, int) or m >= 1:
                    pe.wait_ge(resid_added, 4 * m)
                for r in range(PAIRS):
                    mix(m, r)

            def iteration(n, g, c, first, last_group):
                m = n - 1
                if c == 0:
                    pe.wait_ge(w_low_done, g + 1)
                for j in range(ROPE_TILES):
                    if j == 0 and not first:
                        pe.wait_ge(v_low_done, n)
                    if j == 1 and not first:
                        pe.wait_ge(v_copied, n)
                    if j >= 2:
                        pe.wait_ge(cos_done, ROPE_TILES * n + j - 1)
                    project(j, c)
                if not first:
                    attention_a(m)
                pe.wait_ge(cos_done, ROPE_TILES * n + REP)
                project(REP + 1, c)
                if not first:
                    attention_b(m)
                pe.wait_ge(cos_done, ROPE_TILES * n + ROPE_TILES)
                pe.wait_ge(v_copied, n + 1)
                for r in range(PAIRS):
                    last = nc.tensor.transpose(ps[:, BANK_PROJ, r * P:(r + 1) * P],
                                               v_turn[:, r * P:(r + 1) * P], ident)
                last.then_inc(v_turned, 1)
                if not first:
                    if c == 0:
                        pe.wait_ge(wo_low_done, g)
                    if c == 1:
                        pe.wait_ge(wo_low_done, g + 1)
                    for r in range(PAIRS):
                        out_project(m, r)
                pe.wait_ge(rotated, ROPE_TILES * (n + 1))
                if not first:
                    pe.wait_ge(masked, 2 * n)
                for h in range(2):
                    for b in range(4 * h, 4 * h + 4):
                        for j in range(2):
                            col = (score_columns(b, j) % 8) * T
                            last = mm(ps[:, BANK_SCORE + h, col:col + T],
                                      q_rot[:, j, b, :, :].rearrange("p a t -> p (a t)"),
                                      k_rot[:, b * T:(b + 1) * T], start=True, stop=True)
                    last.then_inc(scored, 1)

            def finish(n):
                m = n - 1
                attention_a(m)
                attention_b(m)
                for r in range(PAIRS):
                    out_project(m, r)

            over_groups(pe, iteration, finish)

            pe.wait_ge(resid_added, 4 * ALL)
            pe.wait_ge(small_loaded, 16 * 13)
            pe.wait_ge(blocks_loaded, 16 * 8)
            pe.wait_ge(sign_step, 3 * KT)

            def step(i, odd, a, b, c, d):
                old = not isinstance(i, int)
                t1, t2, t3 = i - 1, i - 2, i - 3
                o1 = 1 - odd
                if a:
                    pe.wait_ge(ctx_loaded[odd], (i - odd) * 8 + 16 if old else (i // 2) * 16 + 16)
                    if old or i >= 4:
                        pe.wait_ge(out_scale_copied, i - 3)
                    elif i:
                        pe.wait_ge(k_copied, i)
                    for k in range(KT):
                        last = mm(ps[:, 0, k * P:(k + 1) * P], ctx_t[:, odd, k * P:(k + 1) * P],
                                  blocks[:, 1, :], start=True, stop=True)
                    last.then_inc(k_projected, 1)
                    if old or i >= 3:
                        pe.wait_ge(x2_copied, i - 2)
                    elif i:
                        pe.wait_ge(xv_copied, i)
                    mm(ps[:, 1, :], blocks[:, 2, :], ctx_t[:, odd, :], start=True, stop=True)\
                        .then_inc(v_projected, 1)
                if b:
                    pe.wait_ge(x_normed, 2 * t1 + 2)
                    if old or t1 >= 1:
                        pe.wait_ge(sum2_done, t1)
                    for h in range(XH):
                        last = nc.tensor.transpose(ps[:, 2 + h // 4, (h % 4) * P:(h % 4 + 1) * P],
                                                   xdiag[:, h, :], ident)
                        if h % 4 == 3:
                            last.then_inc(diag_turned, 1)
                if d:
                    pe.wait_ge(routed, t3 + 1)
                    nc.tensor.transpose(ps[0:E, 4, 0:P], routing[:, :], ident).then_inc(routing_turned, 1)
                if a:
                    pe.wait_ge(x1_done, i + 1)
                    if old or i >= 3:
                        pe.wait_ge(r_exp_done, i - 2)
                    for k in range(KT):
                        last = mm(ps[:, 5, k * P:(k + 1) * P], x1[:, odd, k * P:(k + 1) * P],
                                  blocks[:, 0, :], start=True, stop=True)
                    last.then_inc(q_projected, 1)
                if b:
                    pe.wait_ge(diag_copied, 2 * t1 + 2)
                    pe.wait_ge(xv_copied, t1 + 1)
                    if old or i >= 4:
                        pe.wait_ge(scaled_done, i - 3)
                    for h in range(XH):
                        l0 = (h % 4) * P + (h // 4) * LH
                        last = mm(ps[:, 6, l0:l0 + LH], xdiag_turn[:, h, :], xv[:, o1, l0:l0 + LH],
                                  start=True, stop=True)
                    last.then_inc(x_mixed, 1)
                if d:
                    pe.wait_ge(routing_copied, t3 + 1)
                    for k in range(KT):
                        last = mm(ps[:, 7, k * P:(k + 1) * P], in_cs[:, k * P:(k + 1) * P],
                                  routing_turn[:, :], start=True, stop=True)
                    last.then_inc(in_scaled, 1)
                    if a:
                        pe.wait_ge(k_copied, i + 1)
                    else:
                        pe.wait_ge(out_scale_copied, t3)
                    mm(ps[:, 0, :], routing_turn[:, :], out_cs[:, :], start=True, stop=True)\
                        .then_inc(out_scale_ready, 1)
                if c:
                    pe.wait_ge(x2_done, t2 + 1)
                    if a:
                        pe.wait_ge(xv_copied, i + 1)
                    else:
                        pe.wait_ge(x2_copied, t2)
                    for k in range(KT):
                        last = nc.tensor.transpose(ps[:, 1, k * P:(k + 1) * P],
                                                   x2[:, odd, k * P:(k + 1) * P], ident)
                    last.then_inc(x2_turned, 1)
                if b:
                    pe.wait_ge(mix_copied, t1 + 1)
                    mm(ps[:, 2, :], blocks[:, 3, :], xmix[:, :], start=True, stop=True).then_inc(cross_done, 1)
                if a:
                    pe.wait_ge(q_copied, 1)
                    pe.wait_ge(k_copied, i + 1)
                    pe.wait_ge(q_copied, i + 1)
                    if d:
                        pe.wait_ge(routing_copied, t3 + 1)
                    for hh in range(2):
                        rows = slice(hh * LH, (hh + 1) * LH)
                        for lt in range(KT):
                            for bb in range(2):
                                cols = slice(bb * T, (bb + 1) * T)
                                last = mm(ps[bb * T:(bb + 1) * T, 3 + hh, lt * LH:(lt + 1) * LH],
                                          xq_turn[rows, lt, cols], xk_turn[rows, lt, cols],
                                          start=True, stop=True)
                    last.then_inc(x_scored, 1)
                if c:
                    pe.wait_ge(x2_copied, t2 + 1)
                    if a:
                        pe.wait_ge(q_copied, i + 1)
                    else:
                        pe.wait_ge(r_exp_done, t2)
                    for k in range(KT):
                        last = mm(ps[:, 5, 0:E], x2_turn[:, odd, k, :], gate_w[:, k, :],
                                  start=(k == 0), stop=(k == KT - 1))
                    last.then_inc(logits_done, 1)
                if d:
                    pe.wait_ge(u_low_done, t3 + 1)
                    if b:
                        pe.wait_ge(mix_copied, t1 + 1)
                    else:
                        pe.wait_ge(scaled_done, t3)
                    for k in range(KT):
                        mm(ps[:, 6, :], u_high[:, k, :], sign_w[:, k, :], start=(k == 0), stop=False)
                        last = mm(ps[:, 6, :], u_low[:, k, :], sign_w[:, k, :], start=False, stop=(k == KT - 1))
                    last.then_inc(signed_done, 1)

            over_tiles(pe, step)

        @block.scalar
        def _(act):
            def copy(dst, src):
                return nc.scalar.activation(dst, src, ACT.Copy)

            for t in range(TILES):
                act.wait_ge(x_turned, t + 1)
                copy(x_high[:, :, t * P:(t + 1) * P],
                     ps[:, t % 8, :].rearrange("p (k t) -> p k t", k=KT)).then_inc(x_high_done, 1)

            def swap(n, c, j):
                slot, bank = (c + j) % 2, BANK_PROJ + j % 2
                act.wait_ge(projected, PROJ_TILES * n + j + 1)
                if not isinstance(n, int) or ROPE_TILES * n + j >= 2:
                    act.wait_ge(rotated, ROPE_TILES * n + j - 1)
                copy(swapped[0:64, slot, :], ps[64:128, bank, :])
                copy(swapped[64:128, slot, :], ps[0:64, bank, :]).then_inc(swap_done, 1)

            def exponential(m):
                for h in range(2):
                    act.wait_ge(shifted, 2 * m + h + 1)
                    half = prob[:, 8 * h:8 * h + 8, :]
                    nc.scalar.activation(half, half, ACT.Exp, scale=ATTN_SCALE).then_inc(exp_done, 1)

            def turn_high(m):
                for h in range(2):
                    act.wait_ge(pt_turned, 2 * m + h + 1)
                    if not isinstance(m, int) or m >= 1:
                        act.wait_ge(mixed, 4 * m)
                    for b in range(2):
                        rows = slice(b * T, (b + 1) * T)
                        last = copy(pt_high[rows, 2 * h:2 * h + 2, b, :],
                                    ps[rows, BANK_TURN + h, :].rearrange("p (q j) -> p q j", q=2))
                    last.then_inc(pt_high_done, 1)

            def mixed_high(m, r):
                bank = (BANK_ACC, BANK_ACC + 1, BANK_TURN, BANK_TURN + 1)[r]
                act.wait_ge(mixed, 4 * m + r + 1)
                if r >= 2 or not isinstance(m, int) or m >= 1:
                    act.wait_ge(out_projected, 4 * m + r - 1)
                src = ps[:, bank, :].rearrange("p (b h t) -> p b h t", b=2, h=REP)
                dst = o_high[:, r % 2, :, :].rearrange("p h (b t) -> p b h t", b=2)
                copy(dst, src).then_inc(o_high_done, 1)

            def iteration(n, g, c, first, last_group):
                m = n - 1
                if first:
                    act.wait_ge(zeroed, 1)
                swap(n, c, 0)
                if not first:
                    exponential(m)
                for j in range(1, ROPE_TILES):
                    swap(n, c, j)
                if not first:
                    turn_high(m)
                act.wait_ge(projected, PROJ_TILES * (n + 1))
                if not first:
                    act.wait_ge(v_turned, n)
                copy(v_turn[:, :], ps[:, BANK_PROJ + 1, :]).then_inc(v_copied, 1)
                if not first:
                    mixed_high(m, 0)
                    mixed_high(m, 1)
                act.wait_ge(v_turned, n + 1)
                if not first:
                    act.wait_ge(mixed, 4 * n)
                copy(v_high[:, :, :], ps[:, BANK_PROJ, :].rearrange("p (r d) -> p r d", r=PAIRS))\
                    .then_inc(v_high_done, 1)
                if not first:
                    mixed_high(m, 2)
                    mixed_high(m, 3)

            def finish(n):
                m = n - 1
                exponential(m)
                turn_high(m)
                for r in range(PAIRS):
                    mixed_high(m, r)

            over_groups(act, iteration, finish)

            act.wait_ge(small_loaded, 16 * 13)

            def step(i, odd, a, b, c, d):
                old = not isinstance(i, int)
                t1, t2, t3 = i - 1, i - 2, i - 3
                o1 = 1 - odd
                if b:
                    act.wait_ge(x_shifted, t1 + 1)
                    nc.scalar.activation(xprob[:, :, :], xprob[:, :, :], ACT.Exp, scale=CROSS_SCALE)\
                        .then_inc(x_exp_done, 1)
                if a:
                    act.wait_ge(v_projected, i + 1)
                    if old or i >= 2:
                        act.wait_ge(x_mixed, i - 1)
                    nc.scalar.activation(xv[:, odd, :], ps[:, 1, :], ACT.Identity, bias=bias_cols[:, 0:1])\
                        .then_inc(xv_copied, 1)
                if d:
                    act.wait_ge(routing_turned, t3 + 1)
                    if old or t3 >= 1:
                        act.wait_ge(out_scale_ready, t3)
                    copy(routing_turn[:, :], ps[0:E, 4, 0:P]).then_inc(routing_copied, 1)
                if b:
                    for h in range(2):
                        act.wait_ge(diag_turned, 2 * t1 + h + 1)
                        if h == 0 and (old or t1 >= 1):
                            act.wait_ge(x_mixed, t1)
                        copy(xdiag_turn[:, 4 * h:4 * h + 4, :],
                             ps[:, 2 + h, :].rearrange("p (h q) -> p h q", h=4)).then_inc(diag_copied, 1)
                    act.wait_ge(x_mixed, t1 + 1)
                    if old or t1 >= 1:
                        act.wait_ge(cross_done, t1)
                    copy(xmix[:, :], ps[:, 6, :]).then_inc(mix_copied, 1)
                if d:
                    act.wait_ge(out_scale_ready, t3 + 1)
                    if old or t3 >= 1:
                        act.wait_ge(scaled_done, t3)
                    copy(out_scale[:, :], ps[:, 0, :]).then_inc(out_scale_copied, 1)
                    act.wait_ge(u_done, t3 + 1)
                    if old or t3 >= 1:
                        act.wait_ge(signed_done, t3)
                    copy(u_high[:, :, :], u[:, :, :]).then_inc(u_high_done, 1)
                if c:
                    act.wait_ge(x2_turned, t2 + 1)
                    if old or t2 >= 2:
                        act.wait_ge(u_done, t2 - 1)
                    copy(x2_turn[:, odd, :, :], ps[:, 1, :].rearrange("p (k t) -> p k t", k=KT))\
                        .then_inc(x2_copied, 1)
                    act.wait_ge(r_max_done, t2 + 1)
                    if old or t2 >= 1:
                        act.wait_ge(routed, t2)
                    nc.scalar.activation(r_exp[:, :], ps[:, 5, 0:E], ACT.Exp, bias=r_max[:, 0:1],
                                         accum_out=r_sum[:, 0:1]).then_inc(r_exp_done, 1)

            over_tiles(act, step)

        @block.vector
        def _(dve):
            v = nc.vector
            v.memset(pt_high[:, :, :, :].bitcast(F32), 0.0)
            v.memset(pt_low[:, :, :, :].bitcast(F32), 0.0).then_inc(zeroed, 1)

            def low(dst, src, high):
                return v.tensor_tensor(dst, src, high, ALU.subtract)

            def split_w_high(g, n):
                dve.wait_ge(wqkv_loaded, 16 * g + 16)
                if n is not None:
                    dve.wait_ge(projected, PROJ_TILES * n)
                v.tensor_copy(w_high[:, :, :], stage[:, :, :]).then_inc(w_high_done, 1)

            def split_wo_high(g, n):
                dve.wait_ge(wo_loaded, 16 * g + 16)
                if n is not None:
                    dve.wait_ge(out_projected, 4 * n)
                v.tensor_copy(wo_high[:, :, :], stage_wo).then_inc(wo_high_done, 1)

            split_w_high(0, None)
            for t in range(TILES):
                dve.wait_ge(x_high_done, t + 1)
                hi = x_high[:, :, t * P:(t + 1) * P]
                low(x_low[:, :, t * P:(t + 1) * P], ps[:, t % 8, :].rearrange("p (k t) -> p k t", k=KT),
                    hi.bitcast(F32)).then_inc(x_low_done, 1)

            def times_cos(n, c, j):
                slot, bank = (c + j) % 2, BANK_PROJ + j % 2
                dve.wait_ge(swap_done, ROPE_TILES * n + j + 1)
                if not isinstance(n, int) or ROPE_TILES * n + j >= 2:
                    dve.wait_ge(rotated, ROPE_TILES * n + j - 1)
                v.tensor_tensor(by_cos[:, slot, :].rearrange("p (b t) -> p b t", t=T),
                                ps[:, bank, :].rearrange("p (b t) -> p b t", t=T),
                                cos.unsqueeze(1).to_broadcast([P, 8, T]), ALU.mult).then_inc(cos_done, 1)

            def shift(m):
                for h in range(2):
                    dve.wait_ge(scored, 2 * m + h + 1)
                    if not isinstance(m, int) or m >= 1:
                        dve.wait_ge(pt_turned, 2 * m)
                    v.tensor_tensor(prob[:, 8 * h:8 * h + 8, :],
                                    ps[:, BANK_SCORE + h, :].rearrange("p (a s) -> p a s", s=T),
                                    causal.unsqueeze(1).to_broadcast([P, 8, T]), ALU.add).then_inc(masked, 1)
                for h in range(2):
                    seg = slice(8 * h, 8 * h + 8)
                    dve.wait_ge(masked, 2 * m + h + 1)
                    v.tensor_reduce(row_max[:, seg], prob[:, seg, :], AX_X, ALU.max).then_inc(max_done, 1)
                for h in range(2):
                    seg = slice(8 * h, 8 * h + 8)
                    dve.wait_ge(max_done, 2 * m + h + 1)
                    v.tensor_tensor(prob[:, seg, :], prob[:, seg, :],
                                    row_max[:, seg].unsqueeze(2).to_broadcast([P, 8, T]),
                                    ALU.subtract).then_inc(shifted, 1)

            def sums(m):
                for h in range(2):
                    seg = slice(8 * h, 8 * h + 8)
                    dve.wait_ge(exp_done, 2 * m + h + 1)
                    v.tensor_reduce(row_sum[:, seg], prob[:, seg, :], AX_X, ALU.add).then_inc(sum_done, 1)
                for h in range(2):
                    seg = slice(8 * h, 8 * h + 8)
                    dve.wait_ge(sum_done, 2 * m + h + 1)
                    v.reciprocal(row_inv[:, seg], row_sum[:, seg]).then_inc(inv_done, 1)

            def turn_low(m):
                for h in range(2):
                    dve.wait_ge(pt_high_done, 2 * m + h + 1)
                    for b in range(2):
                        rows = slice(b * T, (b + 1) * T)
                        last = low(pt_low[rows, 2 * h:2 * h + 2, b, :],
                                   ps[rows, BANK_TURN + h, :].rearrange("p (q j) -> p q j", q=2),
                                   pt_high[rows, 2 * h:2 * h + 2, b, :].bitcast(F32))
                    last.then_inc(pt_low_done, 1)

            def mixed_low(m, r):
                bank = (BANK_ACC, BANK_ACC + 1, BANK_TURN, BANK_TURN + 1)[r]
                dve.wait_ge(o_high_done, 4 * m + r + 1)
                perm = "p h (b t) -> p b h t"
                low(o_low[:, r % 2, :, :].rearrange(perm, b=2),
                    ps[:, bank, :].rearrange("p (b h t) -> p b h t", b=2, h=REP),
                    o_high[:, r % 2, :, :].bitcast(F32).rearrange(perm, b=2)).then_inc(o_low_done, 1)

            def add(m, c, r):
                dve.wait_ge(out_projected, 4 * m + r + 1)
                tile = resid[:, c * PAIRS + r, :]
                v.tensor_tensor(tile, ps[:, BANK_ACC + r % 2, :], tile, ALU.add).then_inc(resid_added, 1)

            def iteration(n, g, c, first, last_group):
                m, mc = n - 1, (c - 1) % CHUNKS
                if not first:
                    shift(m)
                times_cos(n, c, 0)
                times_cos(n, c, 1)
                if not first:
                    sums(m)
                for j in range(2, ROPE_TILES):
                    times_cos(n, c, j)
                if not first:
                    turn_low(m)
                    mixed_low(m, 0)
                    mixed_low(m, 1)
                dve.wait_ge(v_high_done, n + 1)
                low(v_low[:, :, :], ps[:, BANK_PROJ, :].rearrange("p (r d) -> p r d", r=PAIRS),
                    v_high[:, :, :].bitcast(F32)).then_inc(v_low_done, 1)
                if c == CHUNKS - 1 and not last_group:
                    split_w_high(g + 1, n + 1)
                if first:
                    dve.wait_ge(x_turned, TILES)
                    dve.wait_ge(const_loaded, 32)
                    for t in range(TILES):
                        v.tensor_tensor(resid[:, t, :], resid[:, t, :], bo_row, ALU.add).then_inc(biased, 1)
                    dve.wait_ge(biased, TILES)
                else:
                    add(m, mc, 0)
                    mixed_low(m, 2)
                    add(m, mc, 1)
                    mixed_low(m, 3)
                    add(m, mc, 2)
                    add(m, mc, 3)
                if c == 0:
                    split_wo_high(g, None if first else n)

            def finish(n):
                m = n - 1
                shift(m)
                sums(m)
                turn_low(m)
                mixed_low(m, 0)
                mixed_low(m, 1)
                for r in range(PAIRS):
                    add(m, CHUNKS - 1, r)
                    if r < 2:
                        mixed_low(m, r + 2)

            over_groups(dve, iteration, finish)

            dve.wait_ge(projected, ALL * PROJ_TILES)
            v.memset(blocks[:, :, :], 0.0).then_inc(blocks_zeroed, 1)
            v.memset(xdiag[:, :, :], 0.0).then_inc(diag_zeroed, 1)
            v.memset(minus_half[:, :], -0.5).then_inc(diag_zeroed, 1)
            dve.wait_ge(small_loaded, 16 * 13)
            for k in range(KT):
                if k:
                    dve.wait_ge(sign_step, 3 * k)
                v.tensor_scalar(below[:, :], raw_w[:, k, :], 0.0, None, ALU.is_lt).then_inc(sign_step, 1)
                v.tensor_scalar(raw_w[:, k, :], raw_w[:, k, :], 0.0, None, ALU.is_gt).then_inc(sign_step, 1)
                dve.wait_ge(sign_step, 3 * k + 2)
                v.tensor_tensor(sign_w[:, k, :], raw_w[:, k, :], below[:, :], ALU.subtract).then_inc(sign_step, 1)
            dve.wait_ge(resid_added, 4 * ALL)

            def stats_of(k, t, src):
                v.bn_stats(stats[:, k, :], src).then_inc(norm_step[k], 1)

            def stats_landed(k, t):
                dve.wait_ge(norm_step[k], 3 * t + 1)

            def moments_of(k, t):
                v.bn_aggr(moments[:, k, :], stats[:, k, :]).then_inc(norm_step[k], 1)
                dve.wait_ge(norm_step[k], 3 * t + 2)
                v.tensor_scalar(var_eps[:, k:k + 1], moments[:, k, 1:2], EPS, None, ALU.add)\
                    .then_inc(norm_step[k], 1)

            def normalise(k, t, dst, src, done):
                dve.wait_ge(rstd_done[k], t + 1)
                v.tensor_scalar(dst, src, moments[:, k, 0:1], rstd[:, k:k + 1],
                                ALU.subtract, ALU.mult).then_inc(done, 1)

            def resid_tile(i):
                return resid[:, i, :] if isinstance(i, int) else \
                    resid[:, :, :].rearrange("p i c -> p (i c)")[:, bass.ts(i, C)]

            def step(i, odd, a, b, c, d):
                old = not isinstance(i, int)
                t1, t2, t3 = i - 1, i - 2, i - 3
                o1 = 1 - odd
                if b:
                    dve.wait_ge(x_scored, t1 + 1)
                    halves = ps[:, 3:5, 0:KT * LH].rearrange("p a (h e) -> p a h e", e=LH)
                    v.tensor_reduce(x_max[:, :].rearrange("p (a h) -> p a h", a=2), halves, AX_X, ALU.max)\
                        .then_inc(x_max_done, 1)
                if a:
                    stats_of(0, i, resid_tile(i))
                    stats_landed(0, i)
                if b:
                    dve.wait_ge(x_max_done, t1 + 1)
                    for hh in range(2):
                        seg = slice(4 * hh, 4 * hh + 4)
                        last = v.tensor_tensor(
                            xprob[:, seg, :], ps[:, 3 + hh, 0:KT * LH].rearrange("p (h e) -> p h e", e=LH),
                            x_max[:, seg].unsqueeze(2).to_broadcast([P, 4, LH]), ALU.subtract)
                    last.then_inc(x_shifted, 1)
                if a:
                    moments_of(0, i)
                    dve.wait_ge(k_projected, i + 1)
                    if old or i >= 1:
                        dve.wait_ge(x_scored, i)
                    v.tensor_tensor(xk_turn[:, :, :], ps[:, 0, :].rearrange("p (k q) -> p k q", k=KT),
                                    bias_rows[:, 1:2, :].to_broadcast([P, KT, P]), ALU.add).then_inc(k_copied, 1)
                    if old or i >= 2:
                        dve.wait_ge(sum2_done, i - 1)
                    normalise(0, i, x1[:, odd, :], resid_tile(i), x1_done)
                if b:
                    dve.wait_ge(x_exp_done, t1 + 1)
                    v.tensor_reduce(x_sum[:, :], xprob[:, :, :], AX_X, ALU.add).then_inc(x_sum_done, 1)
                    dve.wait_ge(x_sum_done, t1 + 1)
                    v.reciprocal(x_inv[:, :], x_sum[:, :]).then_inc(x_inv_done, 1)
                if a:
                    dve.wait_ge(q_projected, i + 1)
                    v.tensor_tensor(xq_turn[:, :, :], ps[:, 5, :].rearrange("p (k q) -> p k q", k=KT),
                                    bias_rows[:, 0:1, :].to_broadcast([P, KT, P]), ALU.add).then_inc(q_copied, 1)
                if d:
                    dve.wait_ge(in_scaled, t3 + 1)
                    if old or t3 >= 1:
                        dve.wait_ge(u_low_done, t3)
                    v.tensor_tensor(u[:, :, :], ps[:, 7, :].rearrange("p (k t) -> p k t", k=KT),
                                    x2_turn[:, o1, :, :], ALU.mult).then_inc(u_done, 1)
                if b:
                    dve.wait_ge(cross_done, t1 + 1)
                    v.scalar_tensor_tensor(xsum2[:, :], ps[:, 2, :], bias_cols[:, 1:2], x1[:, o1, :],
                                           ALU.add, ALU.add).then_inc(sum2_done, 1)
                    dve.wait_ge(sum2_done, t1 + 1)
                    stats_of(1, t1, xsum2[:, :])
                    stats_landed(1, t1)
                if c:
                    dve.wait_ge(logits_done, t2 + 1)
                    v.tensor_reduce(r_max[:, :], ps[:, 5, 0:E], AX_X, ALU.max, negate=True).then_inc(r_max_done, 1)
                if b:
                    moments_of(1, t1)
                if d:
                    dve.wait_ge(signed_done, t3 + 1)
                    dve.wait_ge(out_scale_copied, t3 + 1)
                    v.tensor_tensor(xsum3[:, :], ps[:, 6, :], out_scale[:, :], ALU.mult).then_inc(scaled_done, 1)
                if b:
                    if old or t1 >= 2:
                        dve.wait_ge(x2_turned, t1 - 1)
                        dve.wait_ge(x2_biased_done, t1 - 1)
                    normalise(1, t1, x2[:, o1, :], xsum2[:, :], x2_done)
                if d:
                    dve.wait_ge(scaled_done, t3 + 1)
                    dve.wait_ge(x2_biased_done, t3 + 1)
                    v.tensor_tensor(xsum3[:, :], xsum3[:, :], x2_biased[:, o1, :], ALU.add).then_inc(sum3_done, 1)
                    dve.wait_ge(sum3_done, t3 + 1)
                    stats_of(2, t3, xsum3[:, :])
                if c:
                    dve.wait_ge(r_exp_done, t2 + 1)
                    v.reciprocal(r_inv[:, :], r_sum[:, :]).then_inc(r_inv_done, 1)
                    if d:
                        stats_landed(2, t3)
                    dve.wait_ge(r_inv_done, t2 + 1)
                    if old or t2 >= 1:
                        dve.wait_ge(routing_turned, t2)
                    v.tensor_scalar(routing[:, :], r_exp[:, :], r_inv[:, 0:1], None, ALU.mult).then_inc(routed, 1)
                elif d:
                    stats_landed(2, t3)
                if d:
                    moments_of(2, t3)
                    if old or t3 >= 2:
                        dve.wait_ge(stored[o1], (i - odd) * 8 - 16 - 16 * (1 - odd) if old
                                    else 16 * (t3 // 2))
                    normalise(2, t3, final[:, o1, :], xsum3[:, :], x3_done)

            over_tiles(dve, step)

        @block.gpsimd
        def _(pool):
            gp = nc.gpsimd

            def split_w_low(g):
                pool.wait_ge(w_high_done, g + 1)
                gp.tensor_tensor(w_low[:, :, :], stage[:, :, :], w_high[:, :, :].bitcast(F32),
                                 ALU.subtract).then_inc(w_low_done, 1)

            def split_wo_low(g):
                pool.wait_ge(wo_high_done, g + 1)
                gp.tensor_tensor(wo_low[:, :, :], stage_wo, wo_high[:, :, :].bitcast(F32),
                                 ALU.subtract).then_inc(wo_low_done, 1)

            def rotate(n, c, j, first):
                slot = (c + j) % 2
                pool.wait_ge(swap_done, ROPE_TILES * n + j + 1)
                part = swapped[:, slot, :].rearrange("p (b t) -> p b t", t=T)
                gp.tensor_tensor(part, part, sin.unsqueeze(1).to_broadcast([P, 8, T]), ALU.mult)\
                    .then_inc(sin_done, 1)
                pool.wait_ge(sin_done, ROPE_TILES * n + j + 1)
                pool.wait_ge(cos_done, ROPE_TILES * n + j + 1)
                if j == 0 and not first:
                    pool.wait_ge(scored, 2 * n)
                dst = k_rot[:, :].rearrange("p (b t) -> p b t", t=T) if j == 0 else \
                    q_rot[:, (j - 1) // 2, :, (j - 1) % 2, :]
                gp.tensor_tensor(dst, by_cos[:, slot, :].rearrange("p (b t) -> p b t", t=T), part,
                                 ALU.add).then_inc(rotated, 1)

            def normalise(m):
                for h in range(2):
                    seg = slice(8 * h, 8 * h + 8)
                    pool.wait_ge(inv_done, 2 * m + h + 1)
                    gp.tensor_tensor(prob[:, seg, :], prob[:, seg, :],
                                     row_inv[:, seg].unsqueeze(2).to_broadcast([P, 8, T]),
                                     ALU.mult).then_inc(normed, 1)

            split_w_low(0)

            def iteration(n, g, c, first, last_group):
                rotate(n, c, 0, first)
                if not first:
                    normalise(n - 1)
                for j in range(1, ROPE_TILES):
                    rotate(n, c, j, first)
                if c == CHUNKS - 1 and not last_group:
                    split_w_low(g + 1)
                if c == 0:
                    split_wo_low(g)

            def finish(n):
                normalise(n - 1)

            over_groups(pool, iteration, finish)

            pool.wait_ge(diag_zeroed, 2)
            pool.wait_ge(small_loaded, 16 * 13)

            def power(k, t):
                pool.wait_ge(norm_step[k], 3 * t + 3)
                gp.tensor_tensor(rstd[:, k:k + 1], var_eps[:, k:k + 1], minus_half[:, :], ALU.pow)\
                    .then_inc(rstd_done[k], 1)

            def step(i, odd, a, b, c, d):
                old = not isinstance(i, int)
                t1, t2, t3 = i - 1, i - 2, i - 3
                o1 = 1 - odd
                if a:
                    if old or i >= 1:
                        pool.wait_ge(x1_done, i)
                    power(0, i)
                if b:
                    pool.wait_ge(x_inv_done, t1 + 1)
                    if old or t1 >= 1:
                        pool.wait_ge(diag_turned, 2 * t1)
                    for bb in range(2):
                        rows = slice(bb * T, (bb + 1) * T)
                        gp.tensor_tensor(xdiag[rows, :, bb * T:(bb + 1) * T], xprob[rows, :, :],
                                         x_inv[rows, :].unsqueeze(2).to_broadcast([T, XH, LH]), ALU.mult)\
                            .then_inc(x_normed, 1)
                        pool.wait_ge(x_normed, 2 * t1 + bb + 1)
                if c:
                    pool.wait_ge(x2_done, t2 + 1)
                    if old or t2 >= 2:
                        pool.wait_ge(sum3_done, t2 - 1)
                    gp.tensor_tensor(x2_biased[:, odd, :], x2[:, odd, :], fbias_row[:, :], ALU.add)\
                        .then_inc(x2_biased_done, 1)
                if d:
                    pool.wait_ge(u_high_done, t3 + 1)
                    if old or t3 >= 1:
                        pool.wait_ge(signed_done, t3)
                    gp.tensor_tensor(u_low[:, :, :], u[:, :, :], u_high[:, :, :].bitcast(F32),
                                     ALU.subtract).then_inc(u_low_done, 1)
                if b:
                    power(1, t1)
                if d:
                    power(2, t3)

            over_tiles(pool, step)


def _shape_constants():
    freqs = (1.0 / np.float32(10000.0) ** (np.arange(0, D, 2, dtype=np.float32) / D)).astype(np.float32)
    angle = np.arange(T, dtype=np.float32)[None, :] * freqs[:, None]
    cos, sin = np.cos(angle).astype(np.float32), np.sin(angle).astype(np.float32)
    table = np.zeros((P, CONSTS), np.float32)
    table[:, COS:COS + T] = np.concatenate([cos, cos])
    table[:, SIN:SIN + T] = np.concatenate([-sin, sin])
    late = np.arange(T)[None, :] > (np.arange(P) % T)[:, None]
    table[:, MASK:MASK + T] = np.where(late, np.float32(MASKED), np.float32(0))
    table[:, IDENT:IDENT + P] = np.eye(P, dtype=np.float32)
    return table


def _halves(w, heads):
    return w.reshape(C, heads, D // 2, 2).transpose(0, 1, 3, 2).reshape(C, heads, D)


def kernel(**inputs):
    from concourse import bacc
    from concourse.bass_utils import run_bass_kernel_spmd

    a = {k: np.ascontiguousarray(v) for k, v in inputs.items()}
    wk = _halves(a["L0_attn_Wk"], G).reshape(C, G, 1, D)
    wq = _halves(a["L0_attn_Wq"], G * REP).reshape(C, G, REP, D)
    wv = a["L0_attn_Wv"].reshape(C, G, 1, D)
    wqkv = np.concatenate([wk, wq, wv], axis=2).reshape(KT, P, G, GCOLS).transpose(2, 1, 0, 3)
    wo = a["L0_attn_Wo"].reshape(G, REP, D, C).transpose(0, 2, 1, 3)
    arrays = {
        "x": a["x"].reshape(TOKENS, C), "ctx": a["ctx_4096"].reshape(TOKENS, C),
        "wqkv": wqkv, "wo": wo, "attn_bo": a["L0_attn_bo"], "consts": _shape_constants(),
        "x_wq": a["L0_xattn_Wq"].T, "x_bq": a["L0_xattn_bq"], "x_wk": a["L0_xattn_Wk"].T,
        "x_bk": a["L0_xattn_bk"], "x_wv": a["L0_xattn_Wv"].T, "x_bv": a["L0_xattn_bv"],
        "x_wo": a["L0_xattn_Wo"].T, "x_bo": a["L0_xattn_bo"], "f_w": a["L0_ffn_weight"].T,
        "f_bias": a["L0_ffn_bias"], "f_gate": a["L0_ffn_gate_w"].T,
        "f_in": a["L0_ffn_in_channel_scale"], "f_out": a["L0_ffn_out_channel_scale"],
    }
    arrays = {f"in_{k}": np.ascontiguousarray(v) for k, v in arrays.items()}
    nc = bacc.Bacc("TRN2", target_bir_lowering=False, num_devices=1)
    args = [nc.dram_tensor(k, v.shape, mybir.dt.from_np(v.dtype), kind="ExternalInput").ap()
            for k, v in arrays.items()]
    args.append(nc.dram_tensor("out", (TOKENS, C), F32, kind="ExternalOutput").ap())
    decoder_layer(nc, *args)
    result = run_bass_kernel_spmd(nc, [arrays], core_ids=[0])
    return result.results[0]["out"].reshape(B, T, C)
```

```python
from contextlib import ExitStack

import concourse.bass as bass
import numpy as np
from concourse import mybir

ALU = mybir.AluOpType
ACT = mybir.ActivationFunctionType
AX_X = mybir.AxisListType.X
F32 = mybir.dt.float32
F32R = mybir.dt.float32r

P = 128
BANK = 512
B, T, C = 32, 64, 512
TOKENS = B * T
G, REP, D = 8, 4, 128
KT = C // P
CHUNK = 512
CHUNKS = TOKENS // CHUNK
PAIRS = CHUNK // P
TILES = TOKENS // P
GCOLS = (REP + 2) * D
XH, LH = 8, 64
E = 8
EPS = 1e-5
ATTN_SCALE = float(D) ** -0.5
CROSS_SCALE = float(LH) ** -0.5
MASKED = -1e38
PROJ_TILES = REP + 2
ROPE_TILES = REP + 1
COS, SIN, MASK, IDENT, CONSTS = 0, T, 2 * T, 3 * T, 3 * T + P
BANK_PROJ, BANK_SCORE, BANK_TURN, BANK_ACC = 0, 2, 4, 6
(BANK_K, BANK_DIAG, _, BANK_IN, BANK_V, BANK_OUT, BANK_X2, BANK_MIX,
 BANK_SIGN, BANK_LOGIT, BANK_Q, BANK_CROSS, BANK_XS, _, BANK_ROUTE) = (k % 8 for k in range(15))


def decoder_layer(nc, x, ctx, wqkv, wo, attn_bo, consts, x_wq, x_bq, x_wk, x_bk, x_wv, x_bv,
                  x_wo, x_bo, f_w, f_bias, f_gate, f_in, f_out, out):
    outer = ExitStack()
    with outer:
        def sem(name):
            return outer.enter_context(nc.semaphore(name))

        def sb(stack, name, shape, dt=F32):
            return stack.enter_context(nc.sbuf_tensor(name, shape, dt))

        ps = outer.enter_context(nc.psum_tensor("ps", [P, 8, BANK], F32))
        resid = sb(outer, "resid", [P, TILES, C])
        const = sb(outer, "const", [P, CONSTS])
        cos, sin = const[:, COS:COS + T], const[:, SIN:SIN + T]
        causal, ident = const[:, MASK:MASK + T], const[:, IDENT:IDENT + P]

        one = ExitStack()
        x_high = sb(one, "x_high", [P, KT, TOKENS], F32R)
        x_low = sb(one, "x_low", [P, KT, TOKENS], F32R)
        w_high = sb(one, "w_high", [P, KT, GCOLS], F32R)
        w_low = sb(one, "w_low", [P, KT, GCOLS], F32R)
        wo_high = sb(one, "wo_high", [P, REP, C], F32R)
        wo_low = sb(one, "wo_low", [P, REP, C], F32R)
        stage = sb(one, "stage", [P, KT, GCOLS])
        q_rot = sb(one, "q_rot", [P, 2, 8, 2, T])
        k_rot = sb(one, "k_rot", [P, CHUNK])
        by_cos = sb(one, "by_cos", [P, 2, CHUNK])
        swapped = sb(one, "swapped", [P, 2, CHUNK])
        prob = sb(one, "prob", [P, 16, T])
        pt_high = sb(one, "pt_high", [P, PAIRS, 2, 2 * P], F32R)
        pt_low = sb(one, "pt_low", [P, PAIRS, 2, 2 * P], F32R)
        v_turn = sb(one, "v_turn", [P, CHUNK])
        v_high = sb(one, "v_high", [P, PAIRS, D], F32R)
        v_low = sb(one, "v_low", [P, PAIRS, D], F32R)
        o_high = sb(one, "o_high", [P, 2, REP, P], F32R)
        o_low = sb(one, "o_low", [P, 2, REP, P], F32R)
        row_max = sb(one, "row_max", [P, 16])
        row_sum = sb(one, "row_sum", [P, 16])
        row_inv = sb(one, "row_inv", [P, 16])
        bo_row = prob[:, 0:8, :].rearrange("p a b -> p (a b)")
        stage_wo = stage[:, :, :].rearrange("p a b -> p (a b)")[:, 0:REP * C].rearrange("p (a b) -> p a b", a=REP)
        one.close()

        two = outer
        ctx_t = sb(two, "ctx_t", [P, 2, C])
        x1 = sb(two, "x1", [P, C])
        x2 = sb(two, "x2", [P, 2, C])
        x2_biased = sb(two, "x2_biased", [P, 2, C])
        x2_turn = sb(two, "x2_turn", [P, 2, KT, P])
        xq_turn = sb(two, "xq_turn", [P, KT, P])
        xk_turn = sb(two, "xk_turn", [P, KT, P])
        xv = sb(two, "xv", [P, 2, C])
        xprob = sb(two, "xprob", [P, XH, LH])
        xdiag = sb(two, "xdiag", [P, XH, P])
        xdiag_turn = sb(two, "xdiag_turn", [P, XH, P])
        xmix = sb(two, "xmix", [P, C])
        xsum2 = sb(two, "xsum2", [P, C])
        u = sb(two, "u", [P, KT, P])
        u_high = sb(two, "u_high", [P, KT, P], F32R)
        u_low = sb(two, "u_low", [P, KT, P], F32R)
        out_scale = sb(two, "out_scale", [P, C])
        xsum3 = sb(two, "xsum3", [P, C])
        final = sb(two, "final", [P, 2, C])
        sign_w = sb(two, "sign_w", [P, KT, C], F32R)
        raw_w = sb(two, "raw_w", [P, KT, C])
        below = sb(two, "below", [P, C])
        fbias_row = sb(two, "fbias_row", [P, C])
        blocks = sb(two, "blocks", [P, 4, P])
        bias_rows = sb(two, "bias_rows", [P, 2, P])
        bias_cols = sb(two, "bias_cols", [P, 2])
        gate_w = sb(two, "gate_w", [P, KT, E])
        in_cs = sb(two, "in_cs", [E, C])
        out_cs = sb(two, "out_cs", [E, C])
        stats = sb(two, "stats", [P, 3, 6])
        moments = sb(two, "moments", [P, 3, 2])
        var_eps = sb(two, "var_eps", [P, 3])
        rstd = sb(two, "rstd", [P, 3])
        minus_half = sb(two, "minus_half", [P, 1])
        x_max = sb(two, "x_max", [P, XH])
        x_sum = sb(two, "x_sum", [P, XH])
        x_inv = sb(two, "x_inv", [P, XH])
        r_max = sb(two, "r_max", [P, 1])
        r_exp = sb(two, "r_exp", [P, E])
        r_sum = sb(two, "r_sum", [P, 1])
        r_inv = sb(two, "r_inv", [P, 1])
        routing = sb(two, "routing", [P, E])
        routing_turn = sb(two, "routing_turn", [E, P])

        x_loaded = [sem(f"x_loaded{c}") for c in range(CHUNKS)]
        const_loaded = sem("const_loaded")
        wqkv_loaded, wo_loaded = sem("wqkv_loaded"), sem("wo_loaded")
        x_turned, x_high_done, x_low_done = sem("x_turned"), sem("x_high_done"), sem("x_low_done")
        zeroed, biased = sem("zeroed"), sem("biased")
        w_high_done, w_low_done = sem("w_high_done"), sem("w_low_done")
        wo_high_done, wo_low_done = sem("wo_high_done"), sem("wo_low_done")
        projected = sem("projected")
        swap_done, cos_done, sin_done, rotated = sem("swap_done"), sem("cos_done"), sem("sin_done"), sem("rotated")
        scored, masked, max_done, shifted = sem("scored"), sem("masked"), sem("max_done"), sem("shifted")
        exp_done, sum_done, inv_done, normed = sem("exp_done"), sem("sum_done"), sem("inv_done"), sem("normed")
        pt_turned, pt_high_done, pt_low_done = sem("pt_turned"), sem("pt_high_done"), sem("pt_low_done")
        v_copied, v_turned, v_high_done, v_low_done = (
            sem("v_copied"), sem("v_turned"), sem("v_high_done"), sem("v_low_done"))
        mixed, o_high_done, o_low_done = sem("mixed"), sem("o_high_done"), sem("o_low_done")
        out_projected, resid_added = sem("out_projected"), sem("resid_added")

        small_loaded, blocks_loaded = sem("small_loaded"), sem("blocks_loaded")
        ctx_loaded = [sem("ctx_loaded0"), sem("ctx_loaded1")]
        blocks_zeroed, diag_zeroed = sem("blocks_zeroed"), sem("diag_zeroed")
        sign_step = sem("sign_step")
        norm_step = [sem(f"norm_step{k}") for k in (1, 2, 3)]
        rstd_done = [sem(f"rstd_done{k}") for k in (1, 2, 3)]
        x1_done, x1_copied, x2_done, x3_done = sem("x1_done"), sem("x1_copied"), sem("x2_done"), sem("x3_done")
        k_projected, v_projected, q_projected = sem("k_projected"), sem("v_projected"), sem("q_projected")
        k_copied, xv_copied, q_copied = sem("k_copied"), sem("xv_copied"), sem("q_copied")
        x_scored, x_max_done, x_shifted, x_exp_done = (
            sem("x_scored"), sem("x_max_done"), sem("x_shifted"), sem("x_exp_done"))
        x_sum_done, x_inv_done, x_normed = sem("x_sum_done"), sem("x_inv_done"), sem("x_normed")
        diag_turned, diag_copied = sem("diag_turned"), sem("diag_copied")
        x_mixed, mix_copied, cross_done, sum2_done = (
            sem("x_mixed"), sem("mix_copied"), sem("cross_done"), sem("sum2_done"))
        x2_biased_done, x2_turned, x2_copied = sem("x2_biased_done"), sem("x2_turned"), sem("x2_copied")
        logits_done, r_max_done, r_exp_done, r_inv_done, routed = (
            sem("logits_done"), sem("r_max_done"), sem("r_exp_done"), sem("r_inv_done"), sem("routed"))
        routing_turned, routing_copied = sem("routing_turned"), sem("routing_copied")
        in_scaled, u_done, u_high_done, u_low_done = (
            sem("in_scaled"), sem("u_done"), sem("u_high_done"), sem("u_low_done"))
        out_scale_ready, out_scale_copied = sem("out_scale_ready"), sem("out_scale_copied")
        signed_done, scaled_done, sum3_done, stored = (
            sem("signed_done"), sem("scaled_done"), sem("sum3_done"), [sem("stored0"), sem("stored1")])

        block = outer.enter_context(nc.Block())
        ALL = G * CHUNKS

        def over_groups(eng, iteration, finish):
            for c in range(CHUNKS):
                iteration(c, 0, c, c == 0, False)
            with eng.Fori(1, G - 1) as g:
                for c in range(CHUNKS):
                    iteration(g * CHUNKS + c, g, c, False, False)
            for c in range(CHUNKS):
                iteration(ALL - CHUNKS + c, G - 1, c, False, True)
            finish(ALL)

        PEEL, TAIL = 6, 2

        def over_tiles(eng, step):
            def peeled(i):
                step(i, i % 2, *(0 <= i - k < TILES for k in range(-1, 5)))

            for i in range(-1, PEEL):
                peeled(i)
            with eng.Fori(0, (TILES - TAIL - PEEL) // 2) as h:
                for odd in range(2):
                    step(h * 2 + (PEEL + odd), odd, True, True, True, True, True, True)
            for i in range(TILES - TAIL, TILES + 4):
                peeled(i)

        def resid_tile(i):
            return resid[:, i, :] if isinstance(i, int) else \
                resid[:, :, :].rearrange("p i c -> p (i c)")[:, bass.ts(i, C)]

        def score_columns(b, j):
            return (b // 2) * 4 + 2 * j + b % 2

        @block.sync
        def _(sp):
            sp.dma_start(const[:, :], consts).then_inc(const_loaded, 16)
            xt = x.rearrange("(i p) c -> p i c", p=P)
            for c in range(CHUNKS):
                sp.dma_start(resid[:, c * PAIRS:(c + 1) * PAIRS, :],
                             xt[:, c * PAIRS:(c + 1) * PAIRS, :]).then_inc(x_loaded[c], 16)
                if c == 0:
                    sp.dma_start(stage[:, :, :], wqkv[0]).then_inc(wqkv_loaded, 16)
                    sp.dma_start(bo_row, attn_bo.partition_broadcast(P)).then_inc(const_loaded, 16)

            def load_wo(g):
                sp.wait_ge(w_low_done, g + 1)
                sp.dma_start(stage_wo, wo[g]).then_inc(wo_loaded, 16)

            def load_wqkv(g):
                sp.wait_ge(wo_low_done, g)
                sp.dma_start(stage[:, :, :], wqkv[g]).then_inc(wqkv_loaded, 16)

            load_wo(0)
            with sp.Fori(1, G) as g:
                load_wqkv(g)
                load_wo(g)

            sp.wait_ge(projected, ALL * PROJ_TILES)
            sp.dma_start(raw_w[:, :, :], f_w.rearrange("(k p) o -> p k o", p=P)).then_inc(small_loaded, 16)
            sp.dma_start(fbias_row[:, :], f_bias.partition_broadcast(P)).then_inc(small_loaded, 16)
            sp.dma_start(gate_w[:, :, :], f_gate.rearrange("(k p) e -> p k e", p=P)).then_inc(small_loaded, 16)
            sp.dma_start(in_cs[:, :], f_in).then_inc(small_loaded, 16)
            sp.dma_start(out_cs[:, :], f_out).then_inc(small_loaded, 16)
            for k, bias in enumerate((x_bq, x_bk)):
                for b in range(2):
                    sp.dma_start(bias_rows[:, k, b * T:(b + 1) * T],
                                 bias.partition_broadcast(P)).then_inc(small_loaded, 16)
            for k, bias in enumerate((x_bv, x_bo)):
                for b in range(2):
                    sp.dma_start(bias_cols[b * T:(b + 1) * T, k:k + 1],
                                 bias.rearrange("(p o) -> p o", o=1)).then_inc(small_loaded, 16)
            SMALL = 16 * 13
            sp.wait_ge(blocks_zeroed, 1)
            for k, w in enumerate((x_wq, x_wk, x_wv, x_wo)):
                for b in range(2):
                    sp.dma_start(blocks[b * T:(b + 1) * T, k, b * T:(b + 1) * T], w).then_inc(blocks_loaded, 16)

            ct = ctx.rearrange("(i p) c -> i p c", p=P)
            ot = out.rearrange("(i p) c -> i p c", p=P)

            def step(i, odd, n, a, b, c, d, e):
                if a:
                    if not isinstance(i, int) or i >= 2:
                        sp.wait_ge(v_projected, i - 1)
                    sp.dma_start(ctx_t[:, odd, :], ct[i] if isinstance(i, int) else
                                 ctx[bass.ts(i, P), :]).then_inc(ctx_loaded[odd], 16)
                if not isinstance(i, int) or i >= 5:
                    store(i - 5, 1 - odd)

            def store(t, slot):
                sp.wait_ge(x3_done, t + 1)
                sp.dma_start(ot[t] if isinstance(t, int) else out[bass.ts(t, P), :],
                             final[:, slot, :]).then_inc(stored[slot], 16)

            over_tiles(sp, step)
            store(TILES - 1, (TILES - 1) % 2)
            for s in stored:
                sp.wait_ge(s, 16 * TILES // 2)

        @block.tensor
        def _(pe):
            mm = nc.tensor.matmul
            pe.wait_ge(const_loaded, 32)
            for t in range(TILES):
                if t % PAIRS == 0:
                    pe.wait_ge(x_loaded[t // PAIRS], 16)
                if t >= 8:
                    pe.wait_ge(x_low_done, t - 7)
                for k in range(KT):
                    last = nc.tensor.transpose(ps[:, t % 8, k * P:(k + 1) * P],
                                               resid[:, t, k * P:(k + 1) * P], ident)
                last.then_inc(x_turned, 1)
            pe.wait_ge(x_low_done, TILES)

            def project(j, c):
                acc = ps[:, BANK_PROJ + j % 2, :]
                cols = slice(j * D, (j + 1) * D)
                tok = slice(c * CHUNK, (c + 1) * CHUNK)
                for k in range(KT):
                    mm(acc, w_high[:, k, cols], x_high[:, k, tok], start=(k == 0), stop=False)
                    mm(acc, w_high[:, k, cols], x_low[:, k, tok], start=False, stop=False)
                    last = mm(acc, w_low[:, k, cols], x_high[:, k, tok], start=False, stop=(k == KT - 1))
                last.then_inc(projected, 1)

            def turn_probs(m):
                for h in range(2):
                    pe.wait_ge(normed, 2 * m + h + 1)
                    for q in range(2):
                        for j in range(2):
                            seg = (2 * h + q) * 4 + 2 * j
                            last = nc.tensor.transpose(
                                ps[:, BANK_TURN + h, (2 * q + j) * P:(2 * q + j + 1) * P],
                                prob[:, seg:seg + 2, :].rearrange("p a b -> p (a b)"), ident)
                    last.then_inc(pt_turned, 1)

            def mix(m, r):
                bank = (BANK_ACC, BANK_ACC + 1, BANK_TURN, BANK_TURN + 1)[r]
                pe.wait_ge(pt_low_done, 2 * m + r // 2 + 1)
                pe.wait_ge(v_low_done, m + 1)
                if r == 2:
                    pe.wait_ge(pt_low_done, 2 * m + 1)
                rhs_high = pt_high[:, r, :, :].rearrange("p a b -> p (a b)")
                rhs_low = pt_low[:, r, :, :].rearrange("p a b -> p (a b)")
                mm(ps[:, bank, :], v_high[:, r, :], rhs_high, start=True, stop=False)
                mm(ps[:, bank, :], v_high[:, r, :], rhs_low, start=False, stop=False)
                mm(ps[:, bank, :], v_low[:, r, :], rhs_high, start=False, stop=True).then_inc(mixed, 1)

            def out_project(m, r):
                pe.wait_ge(o_low_done, 4 * m + r + 1)
                if r >= 2:
                    pe.wait_ge(resid_added, 4 * m + r - 1)
                acc = ps[:, BANK_ACC + r % 2, :]
                for h in range(REP):
                    mm(acc, o_high[:, r % 2, h, :], wo_high[:, h, :], start=(h == 0), stop=False)
                    mm(acc, o_high[:, r % 2, h, :], wo_low[:, h, :], start=False, stop=False)
                    last = mm(acc, o_low[:, r % 2, h, :], wo_high[:, h, :], start=False, stop=(h == REP - 1))
                last.then_inc(out_projected, 1)

            def attention_a(m):
                if not isinstance(m, int) or m >= 1:
                    pe.wait_ge(o_low_done, 4 * m)
                turn_probs(m)

            def attention_b(m):
                if not isinstance(m, int) or m >= 1:
                    pe.wait_ge(resid_added, 4 * m)
                for r in range(PAIRS):
                    mix(m, r)

            def iteration(n, g, c, first, last_group):
                m = n - 1
                if c == 0:
                    pe.wait_ge(w_low_done, g + 1)
                for j in range(ROPE_TILES):
                    if j == 0 and not first:
                        pe.wait_ge(v_low_done, n)
                    if j == 1 and not first:
                        pe.wait_ge(v_copied, n)
                    if j >= 2:
                        pe.wait_ge(cos_done, ROPE_TILES * n + j - 1)
                    project(j, c)
                    if j == REP - 1 and not first:
                        attention_a(m)
                pe.wait_ge(cos_done, ROPE_TILES * n + REP)
                project(REP + 1, c)
                if not first:
                    attention_b(m)
                pe.wait_ge(cos_done, ROPE_TILES * n + ROPE_TILES)
                pe.wait_ge(v_copied, n + 1)
                for r in range(PAIRS):
                    last = nc.tensor.transpose(ps[:, BANK_PROJ, r * P:(r + 1) * P],
                                               v_turn[:, r * P:(r + 1) * P], ident)
                last.then_inc(v_turned, 1)
                if not first:
                    if c == 0:
                        pe.wait_ge(wo_low_done, g)
                    if c == 1:
                        pe.wait_ge(wo_low_done, g + 1)
                    for r in range(PAIRS):
                        out_project(m, r)
                pe.wait_ge(rotated, ROPE_TILES * (n + 1))
                if not first:
                    pe.wait_ge(masked, 2 * n)
                for h in range(2):
                    for b in range(4 * h, 4 * h + 4):
                        for j in range(2):
                            col = (score_columns(b, j) % 8) * T
                            last = mm(ps[:, BANK_SCORE + h, col:col + T],
                                      q_rot[:, j, b, :, :].rearrange("p a t -> p (a t)"),
                                      k_rot[:, b * T:(b + 1) * T], start=True, stop=True)
                    last.then_inc(scored, 1)

            def finish(n):
                m = n - 1
                attention_a(m)
                attention_b(m)
                for r in range(PAIRS):
                    out_project(m, r)

            over_groups(pe, iteration, finish)

            pe.wait_ge(resid_added, 4 * ALL)
            pe.wait_ge(small_loaded, 16 * 13)
            pe.wait_ge(blocks_loaded, 16 * 8)
            pe.wait_ge(sign_step, 3 * KT)

            def step(i, odd, n, a, b, c, d, e):
                old = not isinstance(i, int)
                t0, t1, t2, t3, t4 = i + 1, i - 1, i - 2, i - 3, i - 4
                o1 = 1 - odd
                if a:
                    pe.wait_ge(ctx_loaded[odd], (i - odd) * 8 + 16 if old else (i // 2) * 16 + 16)
                    if old or i >= 5:
                        pe.wait_ge(scaled_done, t4)
                    elif i:
                        pe.wait_ge(k_copied, i)
                    for k in range(KT):
                        last = mm(ps[:, BANK_K, k * P:(k + 1) * P], ctx_t[:, odd, k * P:(k + 1) * P],
                                  blocks[:, 1, :], start=True, stop=True)
                    last.then_inc(k_projected, 1)
                if c:
                    pe.wait_ge(x_normed, 2 * t2 + 2)
                    if old or i >= 4:
                        pe.wait_ge(r_exp_done, t3)
                    elif t2:
                        pe.wait_ge(diag_copied, 2 * t2)
                    for h in range(XH):
                        last = nc.tensor.transpose(
                            ps[:, BANK_DIAG + h // 4, (h % 4) * P:(h % 4 + 1) * P], xdiag[:, h, :], ident)
                        if h % 4 == 3:
                            last.then_inc(diag_turned, 1)
                if e:
                    pe.wait_ge(routing_copied, t4 + 1)
                    pe.wait_ge(sum2_done, min(i - 2, TILES) if not old else i - 2)
                    for k in range(KT):
                        last = mm(ps[:, BANK_IN, k * P:(k + 1) * P], in_cs[:, k * P:(k + 1) * P],
                                  routing_turn[:, :], start=True, stop=True)
                    last.then_inc(in_scaled, 1)
                if a:
                    if old or i >= 1:
                        pe.wait_ge(x_shifted, i)
                    mm(ps[:, BANK_V, :], blocks[:, 2, :], ctx_t[:, odd, :], start=True, stop=True)\
                        .then_inc(v_projected, 1)
                if e:
                    pe.wait_ge(x_shifted, i if old else min(i, TILES))
                    if old or t4 >= 1:
                        pe.wait_ge(out_scale_copied, t4)
                    mm(ps[:, BANK_OUT, :], routing_turn[:, :], out_cs[:, :], start=True, stop=True)\
                        .then_inc(out_scale_ready, 1)
                if d:
                    pe.wait_ge(x2_done, t3 + 1)
                    if old or t3 >= 1:
                        pe.wait_ge(routing_copied, t3)
                    for k in range(KT):
                        last = nc.tensor.transpose(ps[:, BANK_X2, k * P:(k + 1) * P],
                                                   x2[:, o1, k * P:(k + 1) * P], ident)
                    last.then_inc(x2_turned, 1)
                if c:
                    pe.wait_ge(diag_copied, 2 * t2 + 2)
                    pe.wait_ge(xv_copied, t2 + 1)
                    if old or t2 >= 1:
                        pe.wait_ge(mix_copied, t2)
                    for h in range(XH):
                        l0 = (h % 4) * P + (h // 4) * LH
                        last = mm(ps[:, BANK_MIX, l0:l0 + LH], xdiag_turn[:, h, :], xv[:, odd, l0:l0 + LH],
                                  start=True, stop=True)
                    last.then_inc(x_mixed, 1)
                if a:
                    pe.wait_ge(x1_copied, i + 1)
                    if not old and 1 <= i < 2:
                        pe.wait_ge(q_copied, i)
                    for k in range(KT):
                        last = mm(ps[:, BANK_Q, k * P:(k + 1) * P], x1[:, k * P:(k + 1) * P],
                                  blocks[:, 0, :], start=True, stop=True)
                    last.then_inc(q_projected, 1)
                if e:
                    pe.wait_ge(u_low_done, t4 + 1)
                    if a:
                        pe.wait_ge(k_copied, i + 1)
                    elif t4 >= 1:
                        pe.wait_ge(scaled_done, t4)
                    for k in range(KT):
                        mm(ps[:, BANK_SIGN, :], u_high[:, k, :], sign_w[:, k, :], start=(k == 0), stop=False)
                        last = mm(ps[:, BANK_SIGN, :], u_low[:, k, :], sign_w[:, k, :], start=False,
                                  stop=(k == KT - 1))
                    last.then_inc(signed_done, 1)
                if d:
                    pe.wait_ge(x2_copied, t3 + 1)
                    if not c:
                        pe.wait_ge(r_exp_done, t3)
                    for k in range(KT):
                        last = mm(ps[:, BANK_LOGIT, 0:E], x2_turn[:, o1, k, :], gate_w[:, k, :],
                                  start=(k == 0), stop=(k == KT - 1))
                    last.then_inc(logits_done, 1)
                if c:
                    pe.wait_ge(mix_copied, t2 + 1)
                    if e:
                        pe.wait_ge(u_done, t4 + 1)
                    elif t2:
                        pe.wait_ge(sum2_done, t2)
                    mm(ps[:, BANK_CROSS, :], blocks[:, 3, :], xmix[:, :], start=True, stop=True)\
                        .then_inc(cross_done, 1)
                if a:
                    pe.wait_ge(q_copied, 1)
                    pe.wait_ge(k_copied, i + 1)
                    pe.wait_ge(q_copied, i + 1)
                    pe.wait_ge(xv_copied, i + 1)
                    if e:
                        pe.wait_ge(out_scale_copied, t4 + 1)
                    elif i:
                        pe.wait_ge(x_shifted, i)
                    for hh in range(2):
                        rows = slice(hh * LH, (hh + 1) * LH)
                        for lt in range(KT):
                            for bb in range(2):
                                cols = slice(bb * T, (bb + 1) * T)
                                last = mm(ps[bb * T:(bb + 1) * T, BANK_XS + hh, lt * LH:(lt + 1) * LH],
                                          xq_turn[rows, lt, cols], xk_turn[rows, lt, cols],
                                          start=True, stop=True)
                    last.then_inc(x_scored, 1)
                if d:
                    pe.wait_ge(routed, t3 + 1)
                    nc.tensor.transpose(ps[0:E, BANK_ROUTE, 0:P], routing[:, :], ident)\
                        .then_inc(routing_turned, 1)

            over_tiles(pe, step)

        @block.scalar
        def _(act):
            def copy(dst, src):
                return nc.scalar.activation(dst, src, ACT.Copy)

            for t in range(TILES):
                act.wait_ge(x_turned, t + 1)
                copy(x_high[:, :, t * P:(t + 1) * P],
                     ps[:, t % 8, :].rearrange("p (k t) -> p k t", k=KT)).then_inc(x_high_done, 1)

            def swap(n, c, j):
                slot, bank = (c + j) % 2, BANK_PROJ + j % 2
                act.wait_ge(projected, PROJ_TILES * n + j + 1)
                if not isinstance(n, int) or ROPE_TILES * n + j >= 2:
                    act.wait_ge(rotated, ROPE_TILES * n + j - 1)
                copy(swapped[0:64, slot, :], ps[64:128, bank, :])
                copy(swapped[64:128, slot, :], ps[0:64, bank, :]).then_inc(swap_done, 1)

            def exponential(m):
                for h in range(2):
                    act.wait_ge(shifted, 2 * m + h + 1)
                    half = prob[:, 8 * h:8 * h + 8, :]
                    nc.scalar.activation(half, half, ACT.Exp, scale=ATTN_SCALE).then_inc(exp_done, 1)

            def turn_high(m):
                for h in range(2):
                    act.wait_ge(pt_turned, 2 * m + h + 1)
                    if not isinstance(m, int) or m >= 1:
                        act.wait_ge(mixed, 4 * m)
                    for b in range(2):
                        rows = slice(b * T, (b + 1) * T)
                        last = copy(pt_high[rows, 2 * h:2 * h + 2, b, :],
                                    ps[rows, BANK_TURN + h, :].rearrange("p (q j) -> p q j", q=2))
                    last.then_inc(pt_high_done, 1)

            def mixed_high(m, r):
                bank = (BANK_ACC, BANK_ACC + 1, BANK_TURN, BANK_TURN + 1)[r]
                act.wait_ge(mixed, 4 * m + r + 1)
                if r >= 2 or not isinstance(m, int) or m >= 1:
                    act.wait_ge(out_projected, 4 * m + r - 1)
                src = ps[:, bank, :].rearrange("p (b h t) -> p b h t", b=2, h=REP)
                dst = o_high[:, r % 2, :, :].rearrange("p h (b t) -> p b h t", b=2)
                copy(dst, src).then_inc(o_high_done, 1)

            def iteration(n, g, c, first, last_group):
                m = n - 1
                if first:
                    act.wait_ge(zeroed, 1)
                swap(n, c, 0)
                if not first:
                    exponential(m)
                for j in range(1, ROPE_TILES):
                    swap(n, c, j)
                    if j == REP - 1 and not first:
                        turn_high(m)
                act.wait_ge(projected, PROJ_TILES * (n + 1))
                if not first:
                    act.wait_ge(v_turned, n)
                copy(v_turn[:, :], ps[:, BANK_PROJ + 1, :]).then_inc(v_copied, 1)
                if not first:
                    mixed_high(m, 0)
                    mixed_high(m, 1)
                act.wait_ge(v_turned, n + 1)
                if not first:
                    act.wait_ge(mixed, 4 * n)
                copy(v_high[:, :, :], ps[:, BANK_PROJ, :].rearrange("p (r d) -> p r d", r=PAIRS))\
                    .then_inc(v_high_done, 1)
                if not first:
                    mixed_high(m, 2)
                    mixed_high(m, 3)

            def finish(n):
                m = n - 1
                exponential(m)
                turn_high(m)
                for r in range(PAIRS):
                    mixed_high(m, r)

            over_groups(act, iteration, finish)

            act.wait_ge(small_loaded, 16 * 13)

            def step(i, odd, n, a, b, c, d, e):
                old = not isinstance(i, int)
                t0, t1, t2, t3, t4 = i + 1, i - 1, i - 2, i - 3, i - 4
                o1 = 1 - odd
                if b:
                    act.wait_ge(x_shifted, t1 + 1)
                    nc.scalar.activation(xprob[:, :, :], xprob[:, :, :], ACT.Exp, scale=CROSS_SCALE)\
                        .then_inc(x_exp_done, 1)
                if c:
                    for h in range(2):
                        act.wait_ge(diag_turned, 2 * t2 + h + 1)
                        if h == 0 and (old or t2 >= 1):
                            act.wait_ge(x_mixed, t2)
                        copy(xdiag_turn[:, 4 * h:4 * h + 4, :],
                             ps[:, BANK_DIAG + h, :].rearrange("p (h q) -> p h q", h=4)).then_inc(diag_copied, 1)
                if a:
                    act.wait_ge(x1_done, i + 1)
                    if old or i >= 1:
                        act.wait_ge(q_projected, i)
                    copy(x1[:, :], resid_tile(i)).then_inc(x1_copied, 1)
                if e:
                    act.wait_ge(u_done, t4 + 1)
                    if old or t4 >= 1:
                        act.wait_ge(signed_done, t4)
                    copy(u_high[:, :, :], u[:, :, :]).then_inc(u_high_done, 1)
                    act.wait_ge(out_scale_ready, t4 + 1)
                    if old or t4 >= 1:
                        act.wait_ge(scaled_done, t4)
                    copy(out_scale[:, :], ps[:, BANK_OUT, :]).then_inc(out_scale_copied, 1)
                if d:
                    act.wait_ge(x2_turned, t3 + 1)
                    if old or t3 >= 2:
                        act.wait_ge(u_done, t3 - 1)
                    copy(x2_turn[:, o1, :, :], ps[:, BANK_X2, :].rearrange("p (k t) -> p k t", k=KT))\
                        .then_inc(x2_copied, 1)
                if c:
                    act.wait_ge(x_mixed, t2 + 1)
                    if old or t2 >= 1:
                        act.wait_ge(cross_done, t2)
                    copy(xmix[:, :], ps[:, BANK_MIX, :]).then_inc(mix_copied, 1)
                if a:
                    act.wait_ge(v_projected, i + 1)
                    if old or i >= 2:
                        act.wait_ge(x_mixed, i - 1)
                    nc.scalar.activation(xv[:, odd, :], ps[:, BANK_V, :], ACT.Identity, bias=bias_cols[:, 0:1])\
                        .then_inc(xv_copied, 1)
                if d:
                    act.wait_ge(r_max_done, t3 + 1)
                    if old or t3 >= 1:
                        act.wait_ge(routed, t3)
                    nc.scalar.activation(r_exp[:, :], ps[:, BANK_LOGIT, 0:E], ACT.Exp, bias=r_max[:, 0:1],
                                         accum_out=r_sum[:, 0:1]).then_inc(r_exp_done, 1)
                    act.wait_ge(routing_turned, t3 + 1)
                    if old or t3 >= 1:
                        act.wait_ge(out_scale_ready, t3)
                    copy(routing_turn[:, :], ps[0:E, BANK_ROUTE, 0:P]).then_inc(routing_copied, 1)

            over_tiles(act, step)

        @block.vector
        def _(dve):
            v = nc.vector
            v.memset(pt_high[:, :, :, :].bitcast(F32), 0.0)
            v.memset(pt_low[:, :, :, :].bitcast(F32), 0.0).then_inc(zeroed, 1)

            def low(dst, src, high):
                return v.tensor_tensor(dst, src, high, ALU.subtract)

            def split_w_high(g, n):
                dve.wait_ge(wqkv_loaded, 16 * g + 16)
                if n is not None:
                    dve.wait_ge(projected, PROJ_TILES * n)
                v.tensor_copy(w_high[:, :, :], stage[:, :, :]).then_inc(w_high_done, 1)

            def split_wo_high(g, n):
                dve.wait_ge(wo_loaded, 16 * g + 16)
                if n is not None:
                    dve.wait_ge(out_projected, 4 * n)
                v.tensor_copy(wo_high[:, :, :], stage_wo).then_inc(wo_high_done, 1)

            split_w_high(0, None)
            for t in range(TILES):
                dve.wait_ge(x_high_done, t + 1)
                hi = x_high[:, :, t * P:(t + 1) * P]
                low(x_low[:, :, t * P:(t + 1) * P], ps[:, t % 8, :].rearrange("p (k t) -> p k t", k=KT),
                    hi.bitcast(F32)).then_inc(x_low_done, 1)

            def times_cos(n, c, j):
                slot, bank = (c + j) % 2, BANK_PROJ + j % 2
                dve.wait_ge(swap_done, ROPE_TILES * n + j + 1)
                if not isinstance(n, int) or ROPE_TILES * n + j >= 2:
                    dve.wait_ge(rotated, ROPE_TILES * n + j - 1)
                v.tensor_tensor(by_cos[:, slot, :].rearrange("p (b t) -> p b t", t=T),
                                ps[:, bank, :].rearrange("p (b t) -> p b t", t=T),
                                cos.unsqueeze(1).to_broadcast([P, 8, T]), ALU.mult).then_inc(cos_done, 1)

            def shift(m):
                for h in range(2):
                    dve.wait_ge(scored, 2 * m + h + 1)
                    if not isinstance(m, int) or m >= 1:
                        dve.wait_ge(pt_turned, 2 * m)
                    v.tensor_tensor(prob[:, 8 * h:8 * h + 8, :],
                                    ps[:, BANK_SCORE + h, :].rearrange("p (a s) -> p a s", s=T),
                                    causal.unsqueeze(1).to_broadcast([P, 8, T]), ALU.add).then_inc(masked, 1)
                for h in range(2):
                    seg = slice(8 * h, 8 * h + 8)
                    dve.wait_ge(masked, 2 * m + h + 1)
                    v.tensor_reduce(row_max[:, seg], prob[:, seg, :], AX_X, ALU.max).then_inc(max_done, 1)
                for h in range(2):
                    seg = slice(8 * h, 8 * h + 8)
                    dve.wait_ge(max_done, 2 * m + h + 1)
                    v.tensor_tensor(prob[:, seg, :], prob[:, seg, :],
                                    row_max[:, seg].unsqueeze(2).to_broadcast([P, 8, T]),
                                    ALU.subtract).then_inc(shifted, 1)

            def sums(m):
                for h in range(2):
                    seg = slice(8 * h, 8 * h + 8)
                    dve.wait_ge(exp_done, 2 * m + h + 1)
                    v.tensor_reduce(row_sum[:, seg], prob[:, seg, :], AX_X, ALU.add).then_inc(sum_done, 1)
                for h in range(2):
                    seg = slice(8 * h, 8 * h + 8)
                    dve.wait_ge(sum_done, 2 * m + h + 1)
                    v.reciprocal(row_inv[:, seg], row_sum[:, seg]).then_inc(inv_done, 1)

            def normalise_probs(m):
                for h in range(2):
                    seg = slice(8 * h, 8 * h + 8)
                    dve.wait_ge(inv_done, 2 * m + h + 1)
                    v.tensor_tensor(prob[:, seg, :], prob[:, seg, :],
                                    row_inv[:, seg].unsqueeze(2).to_broadcast([P, 8, T]),
                                    ALU.mult).then_inc(normed, 1)

            def turn_low(m):
                for h in range(2):
                    dve.wait_ge(pt_high_done, 2 * m + h + 1)
                    for b in range(2):
                        rows = slice(b * T, (b + 1) * T)
                        last = low(pt_low[rows, 2 * h:2 * h + 2, b, :],
                                   ps[rows, BANK_TURN + h, :].rearrange("p (q j) -> p q j", q=2),
                                   pt_high[rows, 2 * h:2 * h + 2, b, :].bitcast(F32))
                    last.then_inc(pt_low_done, 1)

            def mixed_low(m, r):
                bank = (BANK_ACC, BANK_ACC + 1, BANK_TURN, BANK_TURN + 1)[r]
                dve.wait_ge(o_high_done, 4 * m + r + 1)
                perm = "p h (b t) -> p b h t"
                low(o_low[:, r % 2, :, :].rearrange(perm, b=2),
                    ps[:, bank, :].rearrange("p (b h t) -> p b h t", b=2, h=REP),
                    o_high[:, r % 2, :, :].bitcast(F32).rearrange(perm, b=2)).then_inc(o_low_done, 1)

            def add(m, c, r):
                dve.wait_ge(out_projected, 4 * m + r + 1)
                tile = resid[:, c * PAIRS + r, :]
                v.tensor_tensor(tile, ps[:, BANK_ACC + r % 2, :], tile, ALU.add).then_inc(resid_added, 1)

            def iteration(n, g, c, first, last_group):
                m, mc = n - 1, (c - 1) % CHUNKS
                if not first:
                    shift(m)
                times_cos(n, c, 0)
                times_cos(n, c, 1)
                if not first:
                    sums(m)
                    normalise_probs(m)
                for j in range(2, ROPE_TILES):
                    times_cos(n, c, j)
                    if j == REP - 1 and not first:
                        turn_low(m)
                if not first:
                    mixed_low(m, 0)
                    mixed_low(m, 1)
                dve.wait_ge(v_high_done, n + 1)
                low(v_low[:, :, :], ps[:, BANK_PROJ, :].rearrange("p (r d) -> p r d", r=PAIRS),
                    v_high[:, :, :].bitcast(F32)).then_inc(v_low_done, 1)
                if c == CHUNKS - 1 and not last_group:
                    split_w_high(g + 1, n + 1)
                if first:
                    dve.wait_ge(x_turned, TILES)
                    dve.wait_ge(const_loaded, 32)
                    for t in range(TILES):
                        v.tensor_tensor(resid[:, t, :], resid[:, t, :], bo_row, ALU.add).then_inc(biased, 1)
                    dve.wait_ge(biased, TILES)
                else:
                    add(m, mc, 0)
                    mixed_low(m, 2)
                    add(m, mc, 1)
                    mixed_low(m, 3)
                    add(m, mc, 2)
                    add(m, mc, 3)
                if c == 0:
                    split_wo_high(g, None if first else n)

            def finish(n):
                m = n - 1
                shift(m)
                sums(m)
                normalise_probs(m)
                turn_low(m)
                mixed_low(m, 0)
                mixed_low(m, 1)
                for r in range(PAIRS):
                    add(m, CHUNKS - 1, r)
                    if r < 2:
                        mixed_low(m, r + 2)

            over_groups(dve, iteration, finish)

            dve.wait_ge(projected, ALL * PROJ_TILES)
            v.memset(blocks[:, :, :], 0.0).then_inc(blocks_zeroed, 1)
            v.memset(xdiag[:, :, :], 0.0).then_inc(diag_zeroed, 1)
            v.memset(minus_half[:, :], -0.5).then_inc(diag_zeroed, 1)
            dve.wait_ge(small_loaded, 16 * 13)
            for k in range(KT):
                if k:
                    dve.wait_ge(sign_step, 3 * k)
                v.tensor_scalar(below[:, :], raw_w[:, k, :], 0.0, None, ALU.is_lt).then_inc(sign_step, 1)
                v.tensor_scalar(raw_w[:, k, :], raw_w[:, k, :], 0.0, None, ALU.is_gt).then_inc(sign_step, 1)
                dve.wait_ge(sign_step, 3 * k + 2)
                v.tensor_tensor(sign_w[:, k, :], raw_w[:, k, :], below[:, :], ALU.subtract).then_inc(sign_step, 1)
            dve.wait_ge(resid_added, 4 * ALL)

            def stats_of(k, t, src):
                v.bn_stats(stats[:, k, :], src).then_inc(norm_step[k], 1)

            def stats_landed(k, t):
                dve.wait_ge(norm_step[k], 3 * t + 1)

            def moments_of(k, t):
                v.bn_aggr(moments[:, k, :], stats[:, k, :]).then_inc(norm_step[k], 1)
                dve.wait_ge(norm_step[k], 3 * t + 2)
                v.tensor_scalar(var_eps[:, k:k + 1], moments[:, k, 1:2], EPS, None, ALU.add)\
                    .then_inc(norm_step[k], 1)

            def normalise(k, t, dst, src, done):
                dve.wait_ge(rstd_done[k], t + 1)
                v.tensor_scalar(dst, src, moments[:, k, 0:1], rstd[:, k:k + 1],
                                ALU.subtract, ALU.mult).then_inc(done, 1)

            def step(i, odd, n, a, b, c, d, e):
                old = not isinstance(i, int)
                t0, t1, t2, t3, t4 = i + 1, i - 1, i - 2, i - 3, i - 4
                o1 = 1 - odd
                if a:
                    dve.wait_ge(k_projected, i + 1)
                    if old or i >= 1:
                        dve.wait_ge(x_scored, i)
                    v.tensor_tensor(xk_turn[:, :, :], ps[:, BANK_K, :].rearrange("p (k q) -> p k q", k=KT),
                                    bias_rows[:, 1:2, :].to_broadcast([P, KT, P]), ALU.add).then_inc(k_copied, 1)
                if e:
                    dve.wait_ge(in_scaled, t4 + 1)
                    if old or t4 >= 1:
                        dve.wait_ge(u_low_done, t4)
                    v.tensor_tensor(u[:, :, :], ps[:, BANK_IN, :].rearrange("p (k t) -> p k t", k=KT),
                                    x2_turn[:, odd, :, :], ALU.mult).then_inc(u_done, 1)
                if b:
                    dve.wait_ge(x_exp_done, t1 + 1)
                    v.tensor_reduce(x_sum[:, :], xprob[:, :, :], AX_X, ALU.add).then_inc(x_sum_done, 1)
                    dve.wait_ge(x_sum_done, t1 + 1)
                    v.reciprocal(x_inv[:, :], x_sum[:, :]).then_inc(x_inv_done, 1)
                if n:
                    stats_of(0, t0, resid_tile(t0))
                    stats_landed(0, t0)
                if a:
                    dve.wait_ge(q_projected, i + 1)
                    v.tensor_tensor(xq_turn[:, :, :], ps[:, BANK_Q, :].rearrange("p (k q) -> p k q", k=KT),
                                    bias_rows[:, 0:1, :].to_broadcast([P, KT, P]), ALU.add).then_inc(q_copied, 1)
                if n:
                    moments_of(0, t0)
                if e:
                    dve.wait_ge(signed_done, t4 + 1)
                    dve.wait_ge(out_scale_copied, t4 + 1)
                    v.tensor_tensor(xsum3[:, :], ps[:, BANK_SIGN, :], out_scale[:, :], ALU.mult)\
                        .then_inc(scaled_done, 1)
                if d:
                    dve.wait_ge(logits_done, t3 + 1)
                    v.tensor_reduce(r_max[:, :], ps[:, BANK_LOGIT, 0:E], AX_X, ALU.max, negate=True)\
                        .then_inc(r_max_done, 1)
                if e:
                    dve.wait_ge(scaled_done, t4 + 1)
                    dve.wait_ge(x2_biased_done, t4 + 1)
                    v.tensor_tensor(xsum3[:, :], xsum3[:, :], x2_biased[:, odd, :], ALU.add).then_inc(sum3_done, 1)
                if d:
                    dve.wait_ge(r_exp_done, t3 + 1)
                    v.reciprocal(r_inv[:, :], r_sum[:, :]).then_inc(r_inv_done, 1)
                    dve.wait_ge(r_inv_done, t3 + 1)
                    if old or t3 >= 1:
                        dve.wait_ge(routing_turned, t3)
                    v.tensor_scalar(routing[:, :], r_exp[:, :], r_inv[:, 0:1], None, ALU.mult).then_inc(routed, 1)
                if c:
                    dve.wait_ge(cross_done, t2 + 1)
                    v.scalar_tensor_tensor(xsum2[:, :], ps[:, BANK_CROSS, :], bias_cols[:, 1:2], resid_tile(t2),
                                           ALU.add, ALU.add).then_inc(sum2_done, 1)
                if e:
                    dve.wait_ge(sum3_done, t4 + 1)
                    stats_of(2, t4, xsum3[:, :])
                if c:
                    dve.wait_ge(sum2_done, t2 + 1)
                    stats_of(1, t2, xsum2[:, :])
                if e:
                    stats_landed(2, t4)
                if c:
                    stats_landed(1, t2)
                if a:
                    dve.wait_ge(x_scored, i + 1)
                    halves = ps[:, BANK_XS:BANK_XS + 2, 0:KT * LH].rearrange("p a (h e) -> p a h e", e=LH)
                    v.tensor_reduce(x_max[:, :].rearrange("p (a h) -> p a h", a=2), halves, AX_X, ALU.max)\
                        .then_inc(x_max_done, 1)
                    dve.wait_ge(x_max_done, i + 1)
                    if old or i >= 1:
                        dve.wait_ge(x_normed, 2 * i)
                    for hh in range(2):
                        seg = slice(4 * hh, 4 * hh + 4)
                        last = v.tensor_tensor(
                            xprob[:, seg, :],
                            ps[:, BANK_XS + hh, 0:KT * LH].rearrange("p (h e) -> p h e", e=LH),
                            x_max[:, seg].unsqueeze(2).to_broadcast([P, 4, LH]), ALU.subtract)
                    last.then_inc(x_shifted, 1)
                if c:
                    moments_of(1, t2)
                if e:
                    moments_of(2, t4)
                if n:
                    normalise(0, t0, resid_tile(t0), resid_tile(t0), x1_done)
                if c:
                    if old or t2 >= 2:
                        dve.wait_ge(x2_turned, t2 - 1)
                        dve.wait_ge(x2_biased_done, t2 - 1)
                    normalise(1, t2, x2[:, odd, :], xsum2[:, :], x2_done)
                if e:
                    if old or t4 >= 2:
                        dve.wait_ge(stored[odd], (i - odd) * 8 - 32 if old else 16 * (t4 // 2))
                    normalise(2, t4, final[:, odd, :], xsum3[:, :], x3_done)

            over_tiles(dve, step)

        @block.gpsimd
        def _(pool):
            gp = nc.gpsimd

            def split_w_low(g):
                pool.wait_ge(w_high_done, g + 1)
                gp.tensor_tensor(w_low[:, :, :], stage[:, :, :], w_high[:, :, :].bitcast(F32),
                                 ALU.subtract).then_inc(w_low_done, 1)

            def split_wo_low(g):
                pool.wait_ge(wo_high_done, g + 1)
                gp.tensor_tensor(wo_low[:, :, :], stage_wo, wo_high[:, :, :].bitcast(F32),
                                 ALU.subtract).then_inc(wo_low_done, 1)

            def rotate(n, c, j, first):
                slot = (c + j) % 2
                pool.wait_ge(swap_done, ROPE_TILES * n + j + 1)
                part = swapped[:, slot, :].rearrange("p (b t) -> p b t", t=T)
                gp.tensor_tensor(part, part, sin.unsqueeze(1).to_broadcast([P, 8, T]), ALU.mult)\
                    .then_inc(sin_done, 1)
                pool.wait_ge(sin_done, ROPE_TILES * n + j + 1)
                pool.wait_ge(cos_done, ROPE_TILES * n + j + 1)
                if j == 0 and not first:
                    pool.wait_ge(scored, 2 * n)
                dst = k_rot[:, :].rearrange("p (b t) -> p b t", t=T) if j == 0 else \
                    q_rot[:, (j - 1) // 2, :, (j - 1) % 2, :]
                gp.tensor_tensor(dst, by_cos[:, slot, :].rearrange("p (b t) -> p b t", t=T), part,
                                 ALU.add).then_inc(rotated, 1)

            split_w_low(0)

            def iteration(n, g, c, first, last_group):
                rotate(n, c, 0, first)
                for j in range(1, ROPE_TILES):
                    rotate(n, c, j, first)
                if c == CHUNKS - 1 and not last_group:
                    split_w_low(g + 1)
                if c == 0:
                    split_wo_low(g)

            over_groups(pool, iteration, lambda n: None)

            pool.wait_ge(diag_zeroed, 2)
            pool.wait_ge(small_loaded, 16 * 13)

            def power(k, t):
                pool.wait_ge(norm_step[k], 3 * t + 3)
                gp.tensor_tensor(rstd[:, k:k + 1], var_eps[:, k:k + 1], minus_half[:, :], ALU.pow)\
                    .then_inc(rstd_done[k], 1)

            def step(i, odd, n, a, b, c, d, e):
                old = not isinstance(i, int)
                t0, t1, t2, t3, t4 = i + 1, i - 1, i - 2, i - 3, i - 4
                o1 = 1 - odd
                if e:
                    pool.wait_ge(u_high_done, t4 + 1)
                    gp.tensor_tensor(u_low[:, :, :], u[:, :, :], u_high[:, :, :].bitcast(F32),
                                     ALU.subtract).then_inc(u_low_done, 1)
                if b:
                    pool.wait_ge(x_inv_done, t1 + 1)
                    if old or t1 >= 1:
                        pool.wait_ge(diag_turned, 2 * t1)
                    for bb in range(2):
                        rows = slice(bb * T, (bb + 1) * T)
                        gp.tensor_tensor(xdiag[rows, :, bb * T:(bb + 1) * T], xprob[rows, :, :],
                                         x_inv[rows, :].unsqueeze(2).to_broadcast([T, XH, LH]), ALU.mult)\
                            .then_inc(x_normed, 1)
                        pool.wait_ge(x_normed, 2 * t1 + bb + 1)
                if d:
                    pool.wait_ge(x2_done, t3 + 1)
                    if old or t3 >= 2:
                        pool.wait_ge(sum3_done, t3 - 1)
                    gp.tensor_tensor(x2_biased[:, o1, :], x2[:, o1, :], fbias_row[:, :], ALU.add)\
                        .then_inc(x2_biased_done, 1)
                if n:
                    if old or t0 >= 1:
                        pool.wait_ge(x1_done, t0)
                    power(0, t0)
                if c:
                    power(1, t2)
                if e:
                    power(2, t4)

            over_tiles(pool, step)


def _shape_constants():
    freqs = (1.0 / np.float32(10000.0) ** (np.arange(0, D, 2, dtype=np.float32) / D)).astype(np.float32)
    angle = np.arange(T, dtype=np.float32)[None, :] * freqs[:, None]
    cos, sin = np.cos(angle).astype(np.float32), np.sin(angle).astype(np.float32)
    table = np.zeros((P, CONSTS), np.float32)
    table[:, COS:COS + T] = np.concatenate([cos, cos])
    table[:, SIN:SIN + T] = np.concatenate([-sin, sin])
    late = np.arange(T)[None, :] > (np.arange(P) % T)[:, None]
    table[:, MASK:MASK + T] = np.where(late, np.float32(MASKED), np.float32(0))
    table[:, IDENT:IDENT + P] = np.eye(P, dtype=np.float32)
    return table


def _halves(w, heads):
    return w.reshape(C, heads, D // 2, 2).transpose(0, 1, 3, 2).reshape(C, heads, D)


def kernel(**inputs):
    from concourse import bacc
    from concourse.bass_utils import run_bass_kernel_spmd

    a = {k: np.ascontiguousarray(v) for k, v in inputs.items()}
    wk = _halves(a["L0_attn_Wk"], G).reshape(C, G, 1, D)
    wq = _halves(a["L0_attn_Wq"], G * REP).reshape(C, G, REP, D)
    wv = a["L0_attn_Wv"].reshape(C, G, 1, D)
    wqkv = np.concatenate([wk, wq, wv], axis=2).reshape(KT, P, G, GCOLS).transpose(2, 1, 0, 3)
    wo = a["L0_attn_Wo"].reshape(G, REP, D, C).transpose(0, 2, 1, 3)
    arrays = {
        "x": a["x"].reshape(TOKENS, C), "ctx": a["ctx_4096"].reshape(TOKENS, C),
        "wqkv": wqkv, "wo": wo, "attn_bo": a["L0_attn_bo"], "consts": _shape_constants(),
        "x_wq": a["L0_xattn_Wq"].T, "x_bq": a["L0_xattn_bq"], "x_wk": a["L0_xattn_Wk"].T,
        "x_bk": a["L0_xattn_bk"], "x_wv": a["L0_xattn_Wv"].T, "x_bv": a["L0_xattn_bv"],
        "x_wo": a["L0_xattn_Wo"].T, "x_bo": a["L0_xattn_bo"], "f_w": a["L0_ffn_weight"].T,
        "f_bias": a["L0_ffn_bias"], "f_gate": a["L0_ffn_gate_w"].T,
        "f_in": a["L0_ffn_in_channel_scale"], "f_out": a["L0_ffn_out_channel_scale"],
    }
    arrays = {f"in_{k}": np.ascontiguousarray(v) for k, v in arrays.items()}
    nc = bacc.Bacc("TRN2", target_bir_lowering=False, num_devices=1)
    args = [nc.dram_tensor(k, v.shape, mybir.dt.from_np(v.dtype), kind="ExternalInput").ap()
            for k, v in arrays.items()]
    args.append(nc.dram_tensor("out", (TOKENS, C), F32, kind="ExternalOutput").ap())
    decoder_layer(nc, *args)
    result = run_bass_kernel_spmd(nc, [arrays], core_ids=[0])
    return result.results[0]["out"].reshape(B, T, C)
```

```python
from contextlib import ExitStack

import concourse.bass as bass
import numpy as np
from concourse import mybir

ALU = mybir.AluOpType
ACT = mybir.ActivationFunctionType
AX_X = mybir.AxisListType.X
F32 = mybir.dt.float32
F32R = mybir.dt.float32r

P = 128
BANK = 512
B, T, C = 32, 64, 512
TOKENS = B * T
G, REP, D = 8, 4, 128
KT = C // P
CHUNK = 512
CHUNKS = TOKENS // CHUNK
PAIRS = CHUNK // P
TILES = TOKENS // P
GCOLS = (REP + 2) * D
XH, LH = 8, 64
E = 8
PART = 32
PARTS = 3 * PART
EPS = 1e-5
ATTN_SCALE = float(D) ** -0.5
CROSS_SCALE = float(LH) ** -0.5
MASKED = -1e38
PROJ_TILES = REP + 2
ROPE_TILES = REP + 1
COS, SIN, MASK, IDENT, CONSTS = 0, T, 2 * T, 3 * T, 3 * T + P
BANK_PROJ, BANK_SCORE, BANK_TURN, BANK_ACC = 0, 2, 4, 6
(BANK_K, BANK_DIAG, _, BANK_IN, BANK_V, BANK_OUT, BANK_X2, BANK_MIX,
 BANK_SIGN, BANK_LOGIT, BANK_Q, BANK_CROSS, BANK_XS, _, BANK_ROUTE) = (k % 8 for k in range(15))


def decoder_layer(nc, x, ctx, wqkv, wo, attn_bo, consts, x_wq, x_bq, x_wk, x_bk, x_wv, x_bv,
                  x_wo, x_bo, f_w, f_bias, f_gate, f_in, f_out, out):
    outer = ExitStack()
    with outer:
        def sem(name):
            return outer.enter_context(nc.semaphore(name))

        def sb(stack, name, shape, dt=F32):
            return stack.enter_context(nc.sbuf_tensor(name, shape, dt))

        ps = outer.enter_context(nc.psum_tensor("ps", [P, 8, BANK], F32))
        resid = sb(outer, "resid", [P, TILES, C])
        const = sb(outer, "const", [P, CONSTS])
        cos, sin = const[:, COS:COS + T], const[:, SIN:SIN + T]
        causal, ident = const[:, MASK:MASK + T], const[:, IDENT:IDENT + P]

        blocks = sb(outer, "blocks", [P, 4, P])
        bo_row = blocks[:, :, :].rearrange("p a b -> p (a b)")
        bias_rows = sb(outer, "bias_rows", [P, 2, P])
        bias_cols = sb(outer, "bias_cols", [P, 2])

        one = ExitStack()
        x_high = sb(one, "x_high", [P, KT, TOKENS], F32R)
        x_low = sb(one, "x_low", [P, KT, TOKENS], F32R)
        w_high = sb(one, "w_high", [P, KT, GCOLS], F32R)
        w_low = sb(one, "w_low", [P, KT, GCOLS], F32R)
        wo_high = sb(one, "wo_high", [P, REP, C], F32R)
        wo_low = sb(one, "wo_low", [P, REP, C], F32R)
        stage = sb(one, "stage", [P, KT, GCOLS])
        q_rot = sb(one, "q_rot", [P, 2, 8, 2, T])
        k_rot = sb(one, "k_rot", [P, CHUNK])
        by_cos = sb(one, "by_cos", [P, 2, CHUNK])
        swapped = sb(one, "swapped", [P, 2, CHUNK])
        prob = sb(one, "prob", [P, 16, T])
        pt = sb(one, "pt", [P, PAIRS, 2, 2 * P], F32R)
        v_turn = sb(one, "v_turn", [P, CHUNK])
        v_high = sb(one, "v_high", [P, PAIRS, 2, D], F32R)
        v_low = sb(one, "v_low", [P, PAIRS, 2, D], F32R)
        o_high = sb(one, "o_high", [P, 2, REP, P], F32R)
        o_low = sb(one, "o_low", [P, 2, REP, P], F32R)
        row_max = sb(one, "row_max", [P, 16])
        row_sum = sb(one, "row_sum", [P, 16])
        row_inv = sb(one, "row_inv", [P, 16])
        stage_wo = stage[:, :, :].rearrange("p a b -> p (a b)")[:, 0:REP * C].rearrange("p (a b) -> p a b", a=REP)
        one.close()

        two = outer
        ctx_t = sb(two, "ctx_t", [P, 2, C])
        x1 = sb(two, "x1", [P, C])
        x2 = sb(two, "x2", [P, 2, C])
        x2_biased = sb(two, "x2_biased", [P, 2, C])
        x2_turn = sb(two, "x2_turn", [P, 2, KT, P])
        xq_turn = sb(two, "xq_turn", [P, KT, P])
        xk_turn = sb(two, "xk_turn", [P, KT, P])
        xv = sb(two, "xv", [P, 2, C])
        xprob = sb(two, "xprob", [P, XH, LH])
        xdiag = sb(two, "xdiag", [P, XH, P])
        xdiag_turn = sb(two, "xdiag_turn", [P, XH, P])
        xmix = sb(two, "xmix", [P, C])
        xsum2 = sb(two, "xsum2", [P, C])
        u = sb(two, "u", [P, KT, P])
        u_high = sb(two, "u_high", [P, KT, P], F32R)
        u_low = sb(two, "u_low", [P, KT, P], F32R)
        out_scale = sb(two, "out_scale", [P, C])
        xsum3 = sb(two, "xsum3", [P, 2, C])
        final = sb(two, "final", [P, 2, C])
        sign_w = sb(two, "sign_w", [P, KT, C], F32R)
        raw_w = sb(two, "raw_w", [P, KT, C])
        below = sb(two, "below", [P, C])
        fbias_row = sb(two, "fbias_row", [P, C])
        gate_w = sb(two, "gate_w", [P, KT, E])
        scales_raw = sb(two, "scales_raw", [PARTS, 2, C])
        scales = sb(two, "scales", [PARTS, 2, C], F32R)
        stats = sb(two, "stats", [P, 3, 6])
        moments = sb(two, "moments", [P, 3, 2])
        var_eps = sb(two, "var_eps", [P, 3])
        rstd = sb(two, "rstd", [P, 3])
        offset = sb(two, "offset", [P, 3])
        minus_mean = sb(two, "minus_mean", [P, 3])
        norm_const = sb(two, "norm_const", [P, 3])
        x_max = sb(two, "x_max", [P, XH])
        x_sum = sb(two, "x_sum", [P, XH])
        x_inv = sb(two, "x_inv", [P, XH])
        r_max = sb(two, "r_max", [P, 1])
        r_exp = sb(two, "r_exp", [P, E])
        r_sum = sb(two, "r_sum", [P, 1])
        r_inv = sb(two, "r_inv", [P, 1])
        routing = sb(two, "routing", [P, PARTS], F32R)
        routing_turn = sb(two, "routing_turn", [PARTS, P], F32R)

        x_loaded = [sem(f"x_loaded{c}") for c in range(CHUNKS)]
        const_loaded, bo_loaded = sem("const_loaded"), sem("bo_loaded")
        wk_loaded, wqkv_loaded, wo_loaded = sem("wk_loaded"), sem("wqkv_loaded"), sem("wo_loaded")
        x_turned, x_high_done, x_low_done = sem("x_turned"), sem("x_high_done"), sem("x_low_done")
        zeroed, biased = sem("zeroed"), sem("biased")
        w_high_done, w_low_done = sem("w_high_done"), sem("w_low_done")
        wo_high_done, wo_low_done = sem("wo_high_done"), sem("wo_low_done")
        projected = sem("projected")
        swap_done, cos_done, sin_done, rotated = sem("swap_done"), sem("cos_done"), sem("sin_done"), sem("rotated")
        scored, masked, max_done, shifted = sem("scored"), sem("masked"), sem("max_done"), sem("shifted")
        exp_done, sum_done, inv_done, normed = sem("exp_done"), sem("sum_done"), sem("inv_done"), sem("normed")
        pt_turned, pt_high_done, pt_low_done = sem("pt_turned"), sem("pt_high_done"), sem("pt_low_done")
        v_copied, v_turned, v_high_done, v_low_done = (
            sem("v_copied"), sem("v_turned"), sem("v_high_done"), sem("v_low_done"))
        mixed, o_high_done, o_low_done = sem("mixed"), sem("o_high_done"), sem("o_low_done")
        out_projected, resid_added = sem("out_projected"), sem("resid_added")

        small_loaded, blocks_loaded, bias_loaded = sem("small_loaded"), sem("blocks_loaded"), sem("bias_loaded")
        ctx_loaded = [sem("ctx_loaded0"), sem("ctx_loaded1")]
        blocks_zeroed, diag_zeroed = sem("blocks_zeroed"), sem("diag_zeroed")
        sign_step = sem("sign_step")
        scales_zeroed, scales_high, scales_ready = sem("scales_zeroed"), sem("scales_high"), sem("scales_ready")
        routed_high, routing_zeroed, constants_set = sem("routed_high"), sem("routing_zeroed"), sem("constants_set")
        norm_step = [sem(f"norm_step{k}") for k in (1, 2, 3)]
        var_done = [sem(f"var_done{k}") for k in (1, 2, 3)]
        offset_done = [sem(f"offset_done{k}") for k in (1, 2, 3)]
        rstd_done = [sem(f"rstd_done{k}") for k in (1, 2, 3)]
        x1_done, x1_copied, x2_done, x3_done = sem("x1_done"), sem("x1_copied"), sem("x2_done"), sem("x3_done")
        k_projected, v_projected, q_projected = sem("k_projected"), sem("v_projected"), sem("q_projected")
        k_copied, xv_copied, q_copied = sem("k_copied"), sem("xv_copied"), sem("q_copied")
        x_scored, x_max_done, x_shifted, x_exp_done = (
            sem("x_scored"), sem("x_max_done"), sem("x_shifted"), sem("x_exp_done"))
        x_sum_done, x_inv_done, x_normed = sem("x_sum_done"), sem("x_inv_done"), sem("x_normed")
        diag_turned, diag_copied = sem("diag_turned"), sem("diag_copied")
        x_mixed, mix_copied, cross_done, sum2_done = (
            sem("x_mixed"), sem("mix_copied"), sem("cross_done"), sem("sum2_done"))
        x2_biased_done, x2_turned, x2_copied = sem("x2_biased_done"), sem("x2_turned"), sem("x2_copied")
        logits_done, r_max_done, r_exp_done, r_inv_done, routed = (
            sem("logits_done"), sem("r_max_done"), sem("r_exp_done"), sem("r_inv_done"), sem("routed"))
        routing_turned, routing_copied = sem("routing_turned"), sem("routing_copied")
        in_scaled, u_done, u_high_done, u_low_done = (
            sem("in_scaled"), sem("u_done"), sem("u_high_done"), sem("u_low_done"))
        out_scale_ready, out_scale_copied = sem("out_scale_ready"), sem("out_scale_copied")
        signed_done, scaled_done, sum3_done, stored = (
            sem("signed_done"), sem("scaled_done"), sem("sum3_done"), [sem("stored0"), sem("stored1")])

        block = outer.enter_context(nc.Block())
        ALL = G * CHUNKS
        SMALL, BLOCKS, BIASES = 16 * 9, 16 * 8, 16 * 8

        def over_groups(eng, iteration, finish):
            for c in range(CHUNKS):
                iteration(c, 0, c, c == 0, False)
            with eng.Fori(1, G - 1) as g:
                for c in range(CHUNKS):
                    iteration(g * CHUNKS + c, g, c, False, False)
            for c in range(CHUNKS):
                iteration(ALL - CHUNKS + c, G - 1, c, False, True)
            finish(ALL)

        PEEL, TAIL = 8, 2

        def fixed_step(step, i):
            step(i, i % 2, *(0 <= i - k < TILES for k in range(-1, 6)))

        def over_tiles(eng, step, start=2):
            for i in range(start, PEEL):
                fixed_step(step, i)
            with eng.Fori(0, (TILES - TAIL - PEEL) // 2) as h:
                for odd in range(2):
                    step(h * 2 + (PEEL + odd), odd, True, True, True, True, True, True, True)
            for i in range(TILES - TAIL, TILES + 5):
                fixed_step(step, i)

        def resid_tile(i):
            return resid[:, i, :] if isinstance(i, int) else \
                resid[:, :, :].rearrange("p i c -> p (i c)")[:, bass.ts(i, C)]

        def score_columns(b, j):
            return (b // 2) * 4 + 2 * j + b % 2

        @block.sync
        def _(sp):
            sp.dma_start(const[:, :], consts).then_inc(const_loaded, 16)
            xt = x.rearrange("(i p) c -> p i c", p=P)
            sp.dma_start(stage[:, :, 0:D], wqkv[0, :, :, 0:D]).then_inc(wk_loaded, 16)
            for c in range(CHUNKS):
                sp.dma_start(resid[:, c * PAIRS:(c + 1) * PAIRS, :],
                             xt[:, c * PAIRS:(c + 1) * PAIRS, :]).then_inc(x_loaded[c], 16)
                if c == 0:
                    sp.dma_start(stage[:, :, D:GCOLS], wqkv[0, :, :, D:GCOLS]).then_inc(wqkv_loaded, 16)
                    sp.dma_start(bo_row, attn_bo.partition_broadcast(P)).then_inc(bo_loaded, 16)

            def load_wo(g):
                sp.wait_ge(w_low_done, g + PROJ_TILES)
                sp.dma_start(stage_wo, wo[g]).then_inc(wo_loaded, 16)

            def load_wqkv(g):
                sp.wait_ge(wo_low_done, g)
                sp.dma_start(stage[:, :, :], wqkv[g]).then_inc(wqkv_loaded, 16)

            load_wo(0)
            load_wqkv(1)
            for k, bias in enumerate((x_bq, x_bk)):
                for b in range(2):
                    sp.dma_start(bias_rows[:, k, b * T:(b + 1) * T],
                                 bias.partition_broadcast(P)).then_inc(bias_loaded, 16)
            for k, bias in enumerate((x_bv, x_bo)):
                for b in range(2):
                    sp.dma_start(bias_cols[b * T:(b + 1) * T, k:k + 1],
                                 bias.rearrange("(p o) -> p o", o=1)).then_inc(bias_loaded, 16)
            sp.wait_ge(blocks_zeroed, 1)
            for k, w in enumerate((x_wq, x_wk, x_wv, x_wo)):
                for b in range(2):
                    sp.dma_start(blocks[b * T:(b + 1) * T, k, b * T:(b + 1) * T], w).then_inc(blocks_loaded, 16)
            load_wo(1)
            with sp.Fori(2, G) as g:
                load_wqkv(g)
                load_wo(g)

            ct = ctx.rearrange("(i p) c -> i p c", p=P)
            ot = out.rearrange("(i p) c -> i p c", p=P)

            def step(i, odd, n, a, b, c, d, e, f):
                if a:
                    if not isinstance(i, int) or i >= 2:
                        sp.wait_ge(v_projected, i - 1)
                    sp.dma_start(ctx_t[:, odd, :], ct[i] if isinstance(i, int) else
                                 ctx[bass.ts(i, P), :]).then_inc(ctx_loaded[odd], 16)
                if not isinstance(i, int) or i >= 6:
                    store(i - 6, odd)

            def store(t, slot):
                sp.wait_ge(x3_done, t + 1)
                sp.dma_start(ot[t] if isinstance(t, int) else out[bass.ts(t, P), :],
                             final[:, slot, :]).then_inc(stored[slot], 16)

            sp.wait_ge(projected, ALL * PROJ_TILES)
            fixed_step(step, 0)
            fixed_step(step, 1)
            sp.dma_start(raw_w[:, :, :], f_w.rearrange("(k p) o -> p k o", p=P)).then_inc(small_loaded, 16)
            sp.dma_start(gate_w[:, :, :], f_gate.rearrange("(k p) e -> p k e", p=P)).then_inc(small_loaded, 16)
            sp.wait_ge(scales_zeroed, 1)
            for part in range(3):
                for k, scale in enumerate((f_in, f_out)):
                    sp.dma_start(scales_raw[part * PART:part * PART + E, k, :], scale).then_inc(small_loaded, 16)
            sp.dma_start(fbias_row[:, :], f_bias.partition_broadcast(P)).then_inc(small_loaded, 16)
            over_tiles(sp, step)
            store(TILES - 1, (TILES - 1) % 2)
            for s in stored:
                sp.wait_ge(s, 16 * TILES // 2)

        @block.tensor
        def _(pe):
            mm = nc.tensor.matmul
            pe.wait_ge(const_loaded, 16)

            def turn_x(c):
                pe.wait_ge(x_loaded[c], 16)
                for t in range(c * PAIRS, (c + 1) * PAIRS):
                    if t >= 6:
                        pe.wait_ge(x_low_done, t - 5)
                    for k in range(KT):
                        last = nc.tensor.transpose(ps[:, 2 + t % 6, k * P:(k + 1) * P],
                                                   resid[:, t, k * P:(k + 1) * P], ident)
                    last.then_inc(x_turned, 1)

            def project(j, c):
                acc = ps[:, BANK_PROJ + j % 2, :]
                cols = slice(j * D, (j + 1) * D)
                tok = slice(c * CHUNK, (c + 1) * CHUNK)
                for k in range(KT):
                    mm(acc, w_high[:, k, cols], x_high[:, k, tok], start=(k == 0), stop=False)
                    mm(acc, w_high[:, k, cols], x_low[:, k, tok], start=False, stop=False)
                    last = mm(acc, w_low[:, k, cols], x_high[:, k, tok], start=False, stop=(k == KT - 1))
                last.then_inc(projected, 1)

            def turn_probs(m):
                for h in range(2):
                    pe.wait_ge(normed, 2 * m + h + 1)
                    for q in range(2):
                        for j in range(2):
                            seg = (2 * h + q) * 4 + 2 * j
                            last = nc.tensor.transpose(
                                ps[:, BANK_TURN + h, (2 * q + j) * P:(2 * q + j + 1) * P],
                                prob[:, seg:seg + 2, :].rearrange("p a b -> p (a b)"), ident)
                    last.then_inc(pt_turned, 1)

            def mix(m, r):
                bank = (BANK_ACC, BANK_ACC + 1, BANK_TURN, BANK_TURN + 1)[r]
                pe.wait_ge(pt_low_done, 2 * m + r // 2 + 1)
                pe.wait_ge(v_low_done, m + 1)
                for b in range(2):
                    acc = ps[:, bank, b * 2 * P:(b + 1) * 2 * P]
                    mm(acc, v_high[:, r, b, :], pt[:, r, b, :], start=True, stop=False)
                    last = mm(acc, v_low[:, r, b, :], pt[:, r, b, :], start=False, stop=True)
                last.then_inc(mixed, 1)

            def out_project(m, r):
                pe.wait_ge(o_low_done, 4 * m + r + 1)
                if r >= 2:
                    pe.wait_ge(resid_added, 4 * m + r - 1)
                acc = ps[:, BANK_ACC + r % 2, :]
                for h in range(REP):
                    mm(acc, o_high[:, r % 2, h, :], wo_high[:, h, :], start=(h == 0), stop=False)
                    mm(acc, o_high[:, r % 2, h, :], wo_low[:, h, :], start=False, stop=False)
                    last = mm(acc, o_low[:, r % 2, h, :], wo_high[:, h, :], start=False, stop=(h == REP - 1))
                last.then_inc(out_projected, 1)

            def score(n, first):
                pe.wait_ge(rotated, ROPE_TILES * (n + 1))
                if not first:
                    pe.wait_ge(masked, 2 * n)
                for h in range(2):
                    for b in range(4 * h, 4 * h + 4):
                        for j in range(2):
                            col = (score_columns(b, j) % 8) * T
                            last = mm(ps[:, BANK_SCORE + h, col:col + T],
                                      q_rot[:, j, b, :, :].rearrange("p a t -> p (a t)"),
                                      k_rot[:, b * T:(b + 1) * T], start=True, stop=True)
                    last.then_inc(scored, 1)

            def attention_a(m):
                if not isinstance(m, int) or m >= 1:
                    pe.wait_ge(o_low_done, 4 * m)
                turn_probs(m)

            def attention_b(m):
                if not isinstance(m, int) or m >= 1:
                    pe.wait_ge(resid_added, 4 * m)
                for r in range(PAIRS):
                    mix(m, r)

            def iteration(n, g, c, first, last_group):
                m = n - 1
                if c == 0 and not first:
                    pe.wait_ge(w_low_done, g + PROJ_TILES)
                for j in range(ROPE_TILES):
                    if j == 0 and not first:
                        pe.wait_ge(v_low_done, n)
                    if j == 1 and not first:
                        pe.wait_ge(v_copied, n)
                    if j >= 2:
                        pe.wait_ge(cos_done, ROPE_TILES * n + j - 1)
                    if first and j < CHUNKS:
                        turn_x(j)
                    if first and j == 0:
                        pe.wait_ge(x_low_done, PAIRS)
                    if first:
                        pe.wait_ge(w_low_done, j + 1)
                    project(j, c)
                    if j == REP - 1 and not first:
                        attention_a(m)
                pe.wait_ge(cos_done, ROPE_TILES * n + REP)
                if first:
                    pe.wait_ge(w_low_done, PROJ_TILES)
                project(REP + 1, c)
                if not first:
                    attention_b(m)
                pe.wait_ge(cos_done, ROPE_TILES * n + ROPE_TILES)
                pe.wait_ge(v_copied, n + 1)
                for r in range(PAIRS):
                    last = nc.tensor.transpose(ps[:, BANK_PROJ, r * P:(r + 1) * P],
                                               v_turn[:, r * P:(r + 1) * P], ident)
                last.then_inc(v_turned, 1)
                if first:
                    pe.wait_ge(x_low_done, TILES)
                if last_group and c == CHUNKS - 1:
                    score(n, first)
                if not first:
                    if c == 0:
                        pe.wait_ge(wo_low_done, g)
                    if c == 1:
                        pe.wait_ge(wo_low_done, g + 1)
                    for r in range(PAIRS):
                        if r == 3 and last_group and c == CHUNKS - 1:
                            pe.wait_ge(blocks_loaded, BLOCKS)
                            fixed_step(step, 0)
                        out_project(m, r)
                if not (last_group and c == CHUNKS - 1):
                    score(n, first)

            def project_xk(i, odd):
                looped = not isinstance(i, int)
                t4 = i - 4
                pe.wait_ge(ctx_loaded[odd], (i - odd) * 8 + 16 if looped else (i // 2) * 16 + 16)
                if looped or i >= 5:
                    pe.wait_ge(scaled_done, t4)
                elif i:
                    pe.wait_ge(k_copied, i)
                else:
                    pe.wait_ge(v_low_done, ALL)
                    pe.wait_ge(o_low_done, 4 * (ALL - 1))
                for k in range(KT):
                    last = mm(ps[:, BANK_K, k * P:(k + 1) * P], ctx_t[:, odd, k * P:(k + 1) * P],
                              blocks[:, 1, :], start=True, stop=True)
                last.then_inc(k_projected, 1)

            def step(i, odd, n, a, b, c, d, e, f):
                looped = not isinstance(i, int)
                t0, t1, t2, t3, t4, t5 = i + 1, i - 1, i - 2, i - 3, i - 4, i - 5
                o1 = 1 - odd
                if a and (looped or i != 1):
                    project_xk(i, odd)
                if not looped and i == 4:
                    pe.wait_ge(sign_step, 3 * KT)
                    pe.wait_ge(scales_ready, 1)
                if e:
                    pe.wait_ge(routed, t4 + 1)
                    nc.tensor.transpose(ps[0:PARTS, BANK_ROUTE, 0:P], routing[:, :].bitcast(F32), ident)\
                        .then_inc(routing_turned, 1)
                if c:
                    pe.wait_ge(x_normed, 2 * t2 + 2)
                    if looped or i >= 4:
                        pe.wait_ge(r_exp_done, t3)
                    elif t2:
                        pe.wait_ge(diag_copied, 2 * t2)
                    for h in range(XH):
                        last = nc.tensor.transpose(
                            ps[:, BANK_DIAG + h // 4, (h % 4) * P:(h % 4 + 1) * P], xdiag[:, h, :], ident)
                        if h % 4 == 3:
                            last.then_inc(diag_turned, 1)
                if e:
                    pe.wait_ge(routing_copied, t4 + 1)
                    pe.wait_ge(sum2_done, min(i - 2, TILES) if not looped else i - 2)
                    for k in range(KT):
                        last = mm(ps[:, BANK_IN, k * P:(k + 1) * P], scales[:, 0, k * P:(k + 1) * P],
                                  routing_turn[:, :], start=True, stop=True)
                    last.then_inc(in_scaled, 1)
                if a:
                    if looped or i >= 1:
                        pe.wait_ge(x_shifted, i)
                    mm(ps[:, BANK_V, :], blocks[:, 2, :], ctx_t[:, odd, :], start=True, stop=True)\
                        .then_inc(v_projected, 1)
                if e:
                    pe.wait_ge(x_shifted, i if looped else min(i, TILES))
                    if looped or t4 >= 1:
                        pe.wait_ge(out_scale_copied, t4)
                    mm(ps[:, BANK_OUT, :], routing_turn[:, :], scales[:, 1, :], start=True, stop=True)\
                        .then_inc(out_scale_ready, 1)
                if not looped and i == 2:
                    pe.wait_ge(resid_added, 4 * ALL)
                if c:
                    pe.wait_ge(diag_copied, 2 * t2 + 2)
                    pe.wait_ge(xv_copied, t2 + 1)
                    if looped or t2 >= 1:
                        pe.wait_ge(mix_copied, t2)
                    for h in range(XH):
                        l0 = (h % 4) * P + (h // 4) * LH
                        last = mm(ps[:, BANK_MIX, l0:l0 + LH], xdiag_turn[:, h, :], xv[:, odd, l0:l0 + LH],
                                  start=True, stop=True)
                    last.then_inc(x_mixed, 1)
                if d:
                    pe.wait_ge(x2_done, t3 + 1)
                    if looped or t3 >= 1:
                        pe.wait_ge(routing_copied, t3)
                    for k in range(KT):
                        last = nc.tensor.transpose(ps[:, BANK_X2, k * P:(k + 1) * P],
                                                   x2[:, o1, k * P:(k + 1) * P], ident)
                    last.then_inc(x2_turned, 1)
                if a:
                    pe.wait_ge(x1_copied, i + 1)
                    if not looped and i == 1:
                        pe.wait_ge(q_copied, i)
                    if not looped and i == 0:
                        pe.wait_ge(masked, 2 * ALL)
                    for k in range(KT):
                        last = mm(ps[:, BANK_Q, k * P:(k + 1) * P], x1[:, k * P:(k + 1) * P],
                                  blocks[:, 0, :], start=True, stop=True)
                    last.then_inc(q_projected, 1)
                def sign_product():
                    pe.wait_ge(u_low_done, t4 + 1)
                    if a:
                        pe.wait_ge(k_copied, i + 1)
                    elif t4 >= 1:
                        pe.wait_ge(scaled_done, t4)
                    for k in range(KT):
                        mm(ps[:, BANK_SIGN, :], u_high[:, k, :], sign_w[:, k, :], start=(k == 0), stop=False)
                        last = mm(ps[:, BANK_SIGN, :], u_low[:, k, :], sign_w[:, k, :], start=False,
                                  stop=(k == KT - 1))
                    last.then_inc(signed_done, 1)

                def router_logits():
                    pe.wait_ge(x2_copied, t3 + 1)
                    if not c:
                        pe.wait_ge(r_exp_done, t3)
                    for k in range(KT):
                        last = mm(ps[:, BANK_LOGIT, 0:E], x2_turn[:, o1, k, :], gate_w[:, k, :],
                                  start=(k == 0), stop=(k == KT - 1))
                    last.then_inc(logits_done, 1)

                if e and c:
                    sign_product()
                if d:
                    router_logits()
                if e and not c:
                    sign_product()
                if c:
                    pe.wait_ge(mix_copied, t2 + 1)
                    if e:
                        pe.wait_ge(u_done, t4 + 1)
                    elif t2:
                        pe.wait_ge(sum2_done, t2)
                    mm(ps[:, BANK_CROSS, :], blocks[:, 3, :], xmix[:, :], start=True, stop=True)\
                        .then_inc(cross_done, 1)
                if a:
                    if not looped and i == 1:
                        out_project(ALL - 1, 3)
                    pe.wait_ge(q_copied, 1)
                    pe.wait_ge(k_copied, i + 1)
                    pe.wait_ge(q_copied, i + 1)
                    pe.wait_ge(xv_copied, i + 1)
                    if e:
                        pe.wait_ge(out_scale_copied, t4 + 1)
                    elif i:
                        pe.wait_ge(x_shifted, i)
                    for hh in range(2):
                        rows = slice(hh * LH, (hh + 1) * LH)
                        for lt in range(KT):
                            for bb in range(2):
                                cols = slice(bb * T, (bb + 1) * T)
                                last = mm(ps[bb * T:(bb + 1) * T, BANK_XS + hh, lt * LH:(lt + 1) * LH],
                                          xq_turn[rows, lt, cols], xk_turn[rows, lt, cols],
                                          start=True, stop=True)
                    last.then_inc(x_scored, 1)

            def finish(n):
                m = n - 1
                pe.wait_ge(x_shifted, 1)
                attention_a(m)
                project_xk(1, 1)
                attention_b(m)
                for r in range(3):
                    out_project(m, r)
                pe.wait_ge(o_low_done, 4 * ALL)
                fixed_step(step, 1)

            over_groups(pe, iteration, finish)
            pe.wait_ge(small_loaded, SMALL)
            over_tiles(pe, step)

        @block.scalar
        def _(act):
            def copy(dst, src):
                return nc.scalar.activation(dst, src, ACT.Copy)

            def split_x_high(c):
                for t in range(c * PAIRS, (c + 1) * PAIRS):
                    act.wait_ge(x_turned, t + 1)
                    copy(x_high[:, :, t * P:(t + 1) * P],
                         ps[:, 2 + t % 6, :].rearrange("p (k t) -> p k t", k=KT)).then_inc(x_high_done, 1)

            def swap(n, c, j):
                slot, bank = (c + j) % 2, BANK_PROJ + j % 2
                act.wait_ge(projected, PROJ_TILES * n + j + 1)
                if not isinstance(n, int) or ROPE_TILES * n + j >= 2:
                    act.wait_ge(rotated, ROPE_TILES * n + j - 1)
                copy(swapped[0:64, slot, :], ps[64:128, bank, :])
                copy(swapped[64:128, slot, :], ps[0:64, bank, :]).then_inc(swap_done, 1)

            def exponential(m):
                for h in range(2):
                    act.wait_ge(shifted, 2 * m + h + 1)
                    half = prob[:, 8 * h:8 * h + 8, :]
                    nc.scalar.activation(half, half, ACT.Exp, scale=ATTN_SCALE).then_inc(exp_done, 1)

            def turn_high(m):
                for h in range(2):
                    act.wait_ge(pt_turned, 2 * m + h + 1)
                    if not isinstance(m, int) or m >= 1:
                        act.wait_ge(mixed, 4 * m)
                    for b in range(2):
                        rows = slice(b * T, (b + 1) * T)
                        last = copy(pt[rows, 2 * h:2 * h + 2, b, :],
                                    ps[rows, BANK_TURN + h, :].rearrange("p (q j) -> p q j", q=2))
                    last.then_inc(pt_high_done, 1)

            def mixed_high(m, r):
                bank = (BANK_ACC, BANK_ACC + 1, BANK_TURN, BANK_TURN + 1)[r]
                act.wait_ge(mixed, 4 * m + r + 1)
                if r >= 2 or not isinstance(m, int) or m >= 1:
                    act.wait_ge(out_projected, 4 * m + r - 1)
                src = ps[:, bank, :].rearrange("p (b h t) -> p b h t", b=2, h=REP)
                dst = o_high[:, r % 2, :, :].rearrange("p h (b t) -> p b h t", b=2)
                copy(dst, src).then_inc(o_high_done, 1)

            def apply_norm(k, dst, src, done):
                nc.scalar.activation(dst, src, ACT.Identity, bias=offset[:, k:k + 1], scale=rstd[:, k:k + 1])\
                    .then_inc(done, 1)

            def step(i, odd, n, a, b, c, d, e, f):
                looped = not isinstance(i, int)
                t0, t1, t2, t3, t4, t5 = i + 1, i - 1, i - 2, i - 3, i - 4, i - 5
                o1 = 1 - odd
                if e:
                    act.wait_ge(routing_turned, t4 + 1)
                    if looped or t4 >= 1:
                        act.wait_ge(out_scale_ready, t4)
                    copy(routing_turn[:, :], ps[0:PARTS, BANK_ROUTE, 0:P]).then_inc(routing_copied, 1)
                if c:
                    for h in range(2):
                        act.wait_ge(diag_turned, 2 * t2 + h + 1)
                        if h == 0 and (looped or t2 >= 1):
                            act.wait_ge(x_mixed, t2)
                        copy(xdiag_turn[:, 4 * h:4 * h + 4, :],
                             ps[:, BANK_DIAG + h, :].rearrange("p (h q) -> p h q", h=4)).then_inc(diag_copied, 1)
                if b:
                    act.wait_ge(x_shifted, t1 + 1)
                if a:
                    act.wait_ge(x1_done, i + 1)
                    if looped or i >= 1:
                        act.wait_ge(q_projected, i)
                if b:
                    nc.scalar.activation(xprob[:, :, :], xprob[:, :, :], ACT.Exp, scale=CROSS_SCALE)\
                        .then_inc(x_exp_done, 1)
                if a:
                    copy(x1[:, :], resid_tile(i)).then_inc(x1_copied, 1)
                if e:
                    act.wait_ge(u_done, t4 + 1)
                    if looped or t4 >= 1:
                        act.wait_ge(signed_done, t4)
                    copy(u_high[:, :, :], u[:, :, :]).then_inc(u_high_done, 1)
                    act.wait_ge(out_scale_ready, t4 + 1)
                    if looped or t4 >= 1:
                        act.wait_ge(scaled_done, t4)
                    copy(out_scale[:, :], ps[:, BANK_OUT, :]).then_inc(out_scale_copied, 1)
                if c:
                    act.wait_ge(x_mixed, t2 + 1)
                    if looped or t2 >= 1:
                        act.wait_ge(cross_done, t2)
                    copy(xmix[:, :], ps[:, BANK_MIX, :]).then_inc(mix_copied, 1)
                if d:
                    act.wait_ge(x2_turned, t3 + 1)
                    if looped or t3 >= 2:
                        act.wait_ge(u_done, t3 - 1)
                    copy(x2_turn[:, o1, :, :], ps[:, BANK_X2, :].rearrange("p (k t) -> p k t", k=KT))\
                        .then_inc(x2_copied, 1)
                if a:
                    act.wait_ge(v_projected, i + 1)
                    if looped or i >= 2:
                        act.wait_ge(x_mixed, i - 1)
                    nc.scalar.activation(xv[:, odd, :], ps[:, BANK_V, :], ACT.Identity, bias=bias_cols[:, 0:1])\
                        .then_inc(xv_copied, 1)
                if d:
                    act.wait_ge(r_max_done, t3 + 1)
                    if looped or t3 >= 1:
                        act.wait_ge(routed, t3)
                    nc.scalar.activation(r_exp[:, :], ps[:, BANK_LOGIT, 0:E], ACT.Exp, bias=r_max[:, 0:1],
                                         accum_out=r_sum[:, 0:1]).then_inc(r_exp_done, 1)
                if n:
                    act.wait_ge(offset_done[0], t0 + 1)
                if f:
                    if looped or t5 >= 2:
                        act.wait_ge(stored[o1], (i - 6 + odd) * 8 if looped else 16 * (t5 // 2))
                    act.wait_ge(offset_done[2], t5 + 1)
                    apply_norm(2, final[:, o1, :], xsum3[:, o1, :], x3_done)
                if n:
                    apply_norm(0, resid_tile(t0), resid_tile(t0), x1_done)

            def iteration(n, g, c, first, last_group):
                m = n - 1
                if first:
                    split_x_high(0)
                swap(n, c, 0)
                if not first:
                    exponential(m)
                for j in range(1, ROPE_TILES):
                    if first and j < CHUNKS:
                        split_x_high(j)
                    swap(n, c, j)
                    if j == REP - 1 and not first:
                        turn_high(m)
                act.wait_ge(projected, PROJ_TILES * (n + 1))
                if not first:
                    act.wait_ge(v_turned, n)
                copy(v_turn[:, :], ps[:, BANK_PROJ + 1, :]).then_inc(v_copied, 1)
                if not first:
                    mixed_high(m, 0)
                    mixed_high(m, 1)
                act.wait_ge(v_turned, n + 1)
                if not first:
                    act.wait_ge(mixed, 4 * n)
                for b in range(2):
                    rows = slice(b * T, (b + 1) * T)
                    for half in range(2):
                        last = copy(v_high[half * T:(half + 1) * T, :, b, :],
                                    ps[rows, BANK_PROJ, :].rearrange("p (r d) -> p r d", r=PAIRS))
                last.then_inc(v_high_done, 1)
                last_chunk = last_group and c == CHUNKS - 1
                if last_chunk:
                    fixed_step(step, -1)
                if not first:
                    mixed_high(m, 2)
                if last_chunk:
                    exponential(n)
                if not first:
                    mixed_high(m, 3)
                if last_chunk:
                    act.wait_ge(bias_loaded, BIASES)
                    fixed_step(step, 0)

            def finish(n):
                m = n - 1
                act.wait_ge(small_loaded, SMALL)
                act.wait_ge(scales_zeroed, 1)
                copy(scales[:, :, :], scales_raw[:, :, :]).then_inc(scales_high, 1)
                turn_high(m)
                for r in range(PAIRS):
                    mixed_high(m, r)
                fixed_step(step, 1)

            over_groups(act, iteration, finish)

            over_tiles(act, step)

        @block.vector
        def _(dve):
            v = nc.vector
            v.memset(v_low[:, :, :, :].bitcast(F32), 0.0).then_inc(zeroed, 1)

            def low(dst, src, high):
                return v.tensor_tensor(dst, src, high, ALU.subtract)

            def split_w_high(g, n):
                dve.wait_ge(wqkv_loaded, 16 * g + 16)
                if n is not None:
                    dve.wait_ge(projected, PROJ_TILES * n)
                v.tensor_copy(w_high[:, :, :], stage[:, :, :]).then_inc(w_high_done, 1)

            def split_wo_high(g, n):
                dve.wait_ge(wo_loaded, 16 * g + 16)
                if n is not None:
                    dve.wait_ge(out_projected, 4 * n)
                v.tensor_copy(wo_high[:, :, :], stage_wo).then_inc(wo_high_done, 1)

            def split_x_low(c):
                for t in range(c * PAIRS, (c + 1) * PAIRS):
                    dve.wait_ge(x_high_done, t + 1)
                    hi = x_high[:, :, t * P:(t + 1) * P]
                    low(x_low[:, :, t * P:(t + 1) * P],
                        ps[:, 2 + t % 6, :].rearrange("p (k t) -> p k t", k=KT),
                        hi.bitcast(F32)).then_inc(x_low_done, 1)

            def add_bias(c):
                if c == 0:
                    dve.wait_ge(x_turned, TILES)
                    dve.wait_ge(bo_loaded, 16)
                for t in range(c * PAIRS, (c + 1) * PAIRS):
                    v.tensor_tensor(resid[:, t, :], resid[:, t, :], bo_row, ALU.add).then_inc(biased, 1)

            def split_first_w_high(j):
                cols = slice(j * D, (j + 1) * D)
                v.tensor_copy(w_high[:, :, cols], stage[:, :, cols]).then_inc(w_high_done, 1)

            dve.wait_ge(const_loaded, 16)
            dve.wait_ge(wk_loaded, 16)
            split_first_w_high(0)
            split_x_low(0)
            dve.wait_ge(wqkv_loaded, 16)
            for j in range(1, PROJ_TILES):
                split_first_w_high(j)

            def times_cos(n, c, j):
                slot, bank = (c + j) % 2, BANK_PROJ + j % 2
                dve.wait_ge(swap_done, ROPE_TILES * n + j + 1)
                if not isinstance(n, int) or ROPE_TILES * n + j >= 2:
                    dve.wait_ge(rotated, ROPE_TILES * n + j - 1)
                v.tensor_tensor(by_cos[:, slot, :].rearrange("p (b t) -> p b t", t=T),
                                ps[:, bank, :].rearrange("p (b t) -> p b t", t=T),
                                cos.unsqueeze(1).to_broadcast([P, 8, T]), ALU.mult).then_inc(cos_done, 1)

            def shift(m):
                for h in range(2):
                    dve.wait_ge(scored, 2 * m + h + 1)
                    if not isinstance(m, int) or m >= 1:
                        dve.wait_ge(pt_turned, 2 * m)
                    v.tensor_tensor(prob[:, 8 * h:8 * h + 8, :],
                                    ps[:, BANK_SCORE + h, :].rearrange("p (a s) -> p a s", s=T),
                                    causal.unsqueeze(1).to_broadcast([P, 8, T]), ALU.add).then_inc(masked, 1)
                for h in range(2):
                    seg = slice(8 * h, 8 * h + 8)
                    dve.wait_ge(masked, 2 * m + h + 1)
                    v.tensor_reduce(row_max[:, seg], prob[:, seg, :], AX_X, ALU.max).then_inc(max_done, 1)
                for h in range(2):
                    seg = slice(8 * h, 8 * h + 8)
                    dve.wait_ge(max_done, 2 * m + h + 1)
                    v.tensor_tensor(prob[:, seg, :], prob[:, seg, :],
                                    row_max[:, seg].unsqueeze(2).to_broadcast([P, 8, T]),
                                    ALU.subtract).then_inc(shifted, 1)

            def sums(m):
                for h in range(2):
                    seg = slice(8 * h, 8 * h + 8)
                    dve.wait_ge(exp_done, 2 * m + h + 1)
                    v.tensor_reduce(row_sum[:, seg], prob[:, seg, :], AX_X, ALU.add).then_inc(sum_done, 1)
                for h in range(2):
                    seg = slice(8 * h, 8 * h + 8)
                    dve.wait_ge(sum_done, 2 * m + h + 1)
                    v.reciprocal(row_inv[:, seg], row_sum[:, seg]).then_inc(inv_done, 1)

            def normalise_probs(m):
                for h in range(2):
                    seg = slice(8 * h, 8 * h + 8)
                    dve.wait_ge(inv_done, 2 * m + h + 1)
                    v.tensor_tensor(prob[:, seg, :], prob[:, seg, :],
                                    row_inv[:, seg].unsqueeze(2).to_broadcast([P, 8, T]),
                                    ALU.mult).then_inc(normed, 1)

            def turn_low(m):
                for h in range(2):
                    dve.wait_ge(pt_high_done, 2 * m + h + 1)
                    for b in range(2):
                        rows, others = slice(b * T, (b + 1) * T), slice((1 - b) * T, (2 - b) * T)
                        last = low(pt[others, 2 * h:2 * h + 2, b, :],
                                   ps[rows, BANK_TURN + h, :].rearrange("p (q j) -> p q j", q=2),
                                   pt[rows, 2 * h:2 * h + 2, b, :].bitcast(F32))
                    last.then_inc(pt_low_done, 1)

            def mixed_low(m, r):
                bank = (BANK_ACC, BANK_ACC + 1, BANK_TURN, BANK_TURN + 1)[r]
                dve.wait_ge(o_high_done, 4 * m + r + 1)
                perm = "p h (b t) -> p b h t"
                low(o_low[:, r % 2, :, :].rearrange(perm, b=2),
                    ps[:, bank, :].rearrange("p (b h t) -> p b h t", b=2, h=REP),
                    o_high[:, r % 2, :, :].bitcast(F32).rearrange(perm, b=2)).then_inc(o_low_done, 1)

            def add(m, c, r):
                dve.wait_ge(out_projected, 4 * m + r + 1)
                tile = resid[:, c * PAIRS + r, :]
                v.tensor_tensor(tile, ps[:, BANK_ACC + r % 2, :], tile, ALU.add).then_inc(resid_added, 1)

            def stats_of(k, t, src):
                v.bn_stats(stats[:, k, :], src).then_inc(norm_step[k], 1)

            def stats_landed(k, t):
                dve.wait_ge(norm_step[k], 2 * t + 1)
                if not isinstance(t, int) or t >= 1:
                    dve.wait_ge(rstd_done[k], t)
                    if k != 1:
                        dve.wait_ge(offset_done[k], t)

            def moments_of(k):
                v.bn_aggr(moments[:, k, :], stats[:, k, :]).then_inc(norm_step[k], 1)

            def step(i, odd, n, a, b, c, d, e, f):
                looped = not isinstance(i, int)
                t0, t1, t2, t3, t4, t5 = i + 1, i - 1, i - 2, i - 3, i - 4, i - 5
                o1 = 1 - odd
                if a:
                    dve.wait_ge(k_projected, i + 1)
                    if looped or i >= 1:
                        dve.wait_ge(x_scored, i)
                    v.tensor_tensor(xk_turn[:, :, :], ps[:, BANK_K, :].rearrange("p (k q) -> p k q", k=KT),
                                    bias_rows[:, 1:2, :].to_broadcast([P, KT, P]), ALU.add).then_inc(k_copied, 1)
                if d:
                    if looped or t3 >= 2:
                        dve.wait_ge(x2_turned, t3 - 1)
                        dve.wait_ge(x2_biased_done, t3 - 1)
                    dve.wait_ge(rstd_done[1], t3 + 1)
                    v.tensor_scalar(x2[:, o1, :], xsum2[:, :], moments[:, 1, 0:1], rstd[:, 1:2],
                                    ALU.subtract, ALU.mult).then_inc(x2_done, 1)
                if e:
                    dve.wait_ge(in_scaled, t4 + 1)
                    if looped or t4 >= 1:
                        dve.wait_ge(u_low_done, t4)
                    v.tensor_tensor(u[:, :, :], ps[:, BANK_IN, :].rearrange("p (k t) -> p k t", k=KT),
                                    x2_turn[:, odd, :, :], ALU.mult).then_inc(u_done, 1)
                if f and not a:
                    dve.wait_ge(scaled_done, t5 + 1)
                    dve.wait_ge(x2_biased_done, t5 + 1)
                    v.tensor_tensor(xsum3[:, o1, :], xsum3[:, o1, :], x2_biased[:, o1, :], ALU.add)\
                        .then_inc(sum3_done, 1)
                if e and not a:
                    dve.wait_ge(u_high_done, t4 + 1)
                    low(u_low[:, :, :], u[:, :, :], u_high[:, :, :].bitcast(F32)).then_inc(u_low_done, 1)
                if b:
                    dve.wait_ge(x_exp_done, t1 + 1)
                    v.tensor_reduce(x_sum[:, :], xprob[:, :, :], AX_X, ALU.add).then_inc(x_sum_done, 1)
                    dve.wait_ge(x_sum_done, t1 + 1)
                    v.reciprocal(x_inv[:, :], x_sum[:, :]).then_inc(x_inv_done, 1)
                if n:
                    stats_of(0, t0, resid_tile(t0))
                if f:
                    dve.wait_ge(sum3_done, t5 + 1)
                    stats_of(2, t5, xsum3[:, o1, :])
                if n:
                    stats_landed(0, t0)
                if f:
                    stats_landed(2, t5)
                if a:
                    dve.wait_ge(q_projected, i + 1)
                    v.tensor_tensor(xq_turn[:, :, :], ps[:, BANK_Q, :].rearrange("p (k q) -> p k q", k=KT),
                                    bias_rows[:, 0:1, :].to_broadcast([P, KT, P]), ALU.add).then_inc(q_copied, 1)
                if n:
                    moments_of(0)
                if f:
                    moments_of(2)
                def scale_out():
                    dve.wait_ge(signed_done, t4 + 1)
                    dve.wait_ge(out_scale_copied, t4 + 1)
                    if looped or t4 >= 2:
                        dve.wait_ge(x3_done, t4 - 1)
                    v.tensor_tensor(xsum3[:, odd, :], ps[:, BANK_SIGN, :], out_scale[:, :], ALU.mult)\
                        .then_inc(scaled_done, 1)

                if e and c:
                    scale_out()
                if d:
                    dve.wait_ge(logits_done, t3 + 1)
                    v.tensor_reduce(r_max[:, :], ps[:, BANK_LOGIT, 0:E], AX_X, ALU.max, negate=True)\
                        .then_inc(r_max_done, 1)
                if d:
                    dve.wait_ge(r_exp_done, t3 + 1)
                    v.reciprocal(r_inv[:, :], r_sum[:, :]).then_inc(r_inv_done, 1)
                    dve.wait_ge(r_inv_done, t3 + 1)
                    if looped or t3 >= 1:
                        dve.wait_ge(routing_turned, t3)
                    high = routing[:, 0:2 * PART].rearrange("p (a e) -> p a e", a=2)[:, :, 0:E]
                    v.tensor_scalar(high, r_exp[:, :].unsqueeze(1).to_broadcast([P, 2, E]), r_inv[:, 0:1], None,
                                    ALU.mult).then_inc(routed_high, 1)
                    dve.wait_ge(routed_high, t3 + 1)
                    v.scalar_tensor_tensor(routing[:, 2 * PART:2 * PART + E], r_exp[:, :], r_inv[:, 0:1],
                                           routing[:, 0:E].bitcast(F32), ALU.mult, ALU.subtract).then_inc(routed, 1)
                if e and not c:
                    scale_out()
                if c:
                    dve.wait_ge(cross_done, t2 + 1)
                    v.scalar_tensor_tensor(xsum2[:, :], ps[:, BANK_CROSS, :], bias_cols[:, 1:2], resid_tile(t2),
                                           ALU.add, ALU.add).then_inc(sum2_done, 1)
                if c:
                    dve.wait_ge(sum2_done, t2 + 1)
                    stats_of(1, t2, xsum2[:, :])
                if c:
                    stats_landed(1, t2)
                if a:
                    dve.wait_ge(x_scored, i + 1)
                    halves = ps[:, BANK_XS:BANK_XS + 2, 0:KT * LH].rearrange("p a (h e) -> p a h e", e=LH)
                    v.tensor_reduce(x_max[:, :].rearrange("p (a h) -> p a h", a=2), halves, AX_X, ALU.max)\
                        .then_inc(x_max_done, 1)
                    dve.wait_ge(x_max_done, i + 1)
                    if looped or i >= 1:
                        dve.wait_ge(x_normed, 2 * i)
                    for hh in range(2):
                        seg = slice(4 * hh, 4 * hh + 4)
                        last = v.tensor_tensor(
                            xprob[:, seg, :],
                            ps[:, BANK_XS + hh, 0:KT * LH].rearrange("p (h e) -> p h e", e=LH),
                            x_max[:, seg].unsqueeze(2).to_broadcast([P, 4, LH]), ALU.subtract)
                    last.then_inc(x_shifted, 1)
                if c:
                    moments_of(1)

            def sign_tile(k):
                if k:
                    dve.wait_ge(sign_step, 3 * k)
                v.tensor_scalar(below[:, :], raw_w[:, k, :], 0.0, None, ALU.is_lt).then_inc(sign_step, 1)
                v.tensor_scalar(raw_w[:, k, :], raw_w[:, k, :], 0.0, None, ALU.is_gt).then_inc(sign_step, 1)
                dve.wait_ge(sign_step, 3 * k + 2)
                v.tensor_tensor(sign_w[:, k, :], raw_w[:, k, :], below[:, :], ALU.subtract).then_inc(sign_step, 1)

            def iteration(n, g, c, first, last_group):
                m, mc = n - 1, (c - 1) % CHUNKS
                first_group = isinstance(g, int) and g == 0
                last_chunk = last_group and c == CHUNKS - 1
                if not first:
                    shift(m)
                times_cos(n, c, 0)
                if first:
                    split_x_low(1)
                times_cos(n, c, 1)
                if not first:
                    sums(m)
                    normalise_probs(m)
                for j in range(2, ROPE_TILES):
                    if first and j < CHUNKS:
                        split_x_low(j)
                    times_cos(n, c, j)
                    if first and j == REP - 1:
                        add_bias(0)
                    if j == REP - 1 and not first:
                        turn_low(m)
                if not first:
                    mixed_low(m, 0)
                    mixed_low(m, 1)
                dve.wait_ge(v_high_done, n + 1)
                if first:
                    dve.wait_ge(zeroed, 1)
                for b in range(2):
                    rows = slice(b * T, (b + 1) * T)
                    last = low(v_low[rows, :, b, :], ps[rows, BANK_PROJ, :].rearrange("p (r d) -> p r d", r=PAIRS),
                               v_high[rows, :, b, :].bitcast(F32))
                last.then_inc(v_low_done, 1)
                if last_chunk:
                    dve.wait_ge(projected, ALL * PROJ_TILES)
                    fixed_step(step, -1)
                    shift(n)
                if not first:
                    if first_group:
                        dve.wait_ge(biased, n * PAIRS)
                    add(m, mc, 0)
                    mixed_low(m, 2)
                    if c == CHUNKS - 1 and not last_group:
                        split_w_high(g + 1, n + 1)
                    add(m, mc, 1)
                    mixed_low(m, 3)
                    if last_chunk:
                        sums(n)
                        normalise_probs(n)
                        dve.wait_ge(bias_loaded, BIASES)
                        fixed_step(step, 0)
                    add(m, mc, 2)
                    if last_chunk:
                        dve.wait_ge(small_loaded, SMALL)
                        sign_tile(0)
                    add(m, mc, 3)
                if first_group:
                    if c:
                        add_bias(c)
                    if c == CHUNKS - 1:
                        dve.wait_ge(biased, TILES)
                        v.memset(blocks[:, :, :], 0.0).then_inc(blocks_zeroed, 1)
                if c == 0:
                    split_wo_high(g, None if first else n)

            def finish(n):
                m = n - 1
                turn_low(m)
                mixed_low(m, 0)
                mixed_low(m, 1)
                sign_tile(1)
                add(m, CHUNKS - 1, 0)
                mixed_low(m, 2)
                sign_tile(2)
                add(m, CHUNKS - 1, 1)
                mixed_low(m, 3)
                fixed_step(step, 1)
                add(m, CHUNKS - 1, 2)
                add(m, CHUNKS - 1, 3)
                dve.wait_ge(resid_added, 4 * ALL)
                fixed_step(step, 2)
                sign_tile(3)
                dve.wait_ge(routing_zeroed, 1)

            over_groups(dve, iteration, finish)
            over_tiles(dve, step, 3)

        @block.gpsimd
        def _(pool):
            gp = nc.gpsimd

            def split_w_low(g):
                pool.wait_ge(w_high_done, g + PROJ_TILES)
                gp.tensor_tensor(w_low[:, :, :], stage[:, :, :], w_high[:, :, :].bitcast(F32),
                                 ALU.subtract).then_inc(w_low_done, 1)

            def split_wo_low(g):
                pool.wait_ge(wo_high_done, g + 1)
                gp.tensor_tensor(wo_low[:, :, :], stage_wo, wo_high[:, :, :].bitcast(F32),
                                 ALU.subtract).then_inc(wo_low_done, 1)

            def rotate(n, c, j, first):
                slot = (c + j) % 2
                pool.wait_ge(swap_done, ROPE_TILES * n + j + 1)
                part = swapped[:, slot, :].rearrange("p (b t) -> p b t", t=T)
                gp.tensor_tensor(part, part, sin.unsqueeze(1).to_broadcast([P, 8, T]), ALU.mult)\
                    .then_inc(sin_done, 1)
                pool.wait_ge(sin_done, ROPE_TILES * n + j + 1)
                pool.wait_ge(cos_done, ROPE_TILES * n + j + 1)
                if j == 0 and not first:
                    pool.wait_ge(scored, 2 * n)
                dst = k_rot[:, :].rearrange("p (b t) -> p b t", t=T) if j == 0 else \
                    q_rot[:, (j - 1) // 2, :, (j - 1) % 2, :]
                gp.tensor_tensor(dst, by_cos[:, slot, :].rearrange("p (b t) -> p b t", t=T), part,
                                 ALU.add).then_inc(rotated, 1)

            for j in range(PROJ_TILES):
                cols = slice(j * D, (j + 1) * D)
                pool.wait_ge(w_high_done, j + 1)
                gp.tensor_tensor(w_low[:, :, cols], stage[:, :, cols], w_high[:, :, cols].bitcast(F32),
                                 ALU.subtract).then_inc(w_low_done, 1)

            def iteration(n, g, c, first, last_group):
                rotate(n, c, 0, first)
                for j in range(1, ROPE_TILES):
                    rotate(n, c, j, first)
                if c == CHUNKS - 1 and not last_group:
                    split_w_low(g + 1)
                if c == 0:
                    split_wo_low(g)

            over_groups(pool, iteration, lambda n: None)

            pool.wait_ge(projected, ALL * PROJ_TILES)
            gp.memset(scales_raw[:, :, :], 0.0).then_inc(scales_zeroed, 1)
            for k, value in enumerate((EPS, -0.5, -1.0)):
                gp.memset(norm_const[:, k:k + 1], value).then_inc(constants_set, 1)
            gp.memset(routing[:, :].bitcast(F32), 0.0).then_inc(routing_zeroed, 1)
            gp.memset(xdiag[:, :, :], 0.0).then_inc(diag_zeroed, 1)
            pool.wait_ge(constants_set, 3)
            pool.wait_ge(diag_zeroed, 1)

            def power(k, t, used):
                one = slice(k, k + 1)
                pool.wait_ge(norm_step[k], 2 * t + 2)
                if not isinstance(t, int) or t >= 1:
                    pool.wait_ge(used, t)
                gp.tensor_tensor(var_eps[:, one], moments[:, k, 1:2], norm_const[:, 0:1], ALU.add)\
                    .then_inc(var_done[k], 1)
                if k != 1:
                    gp.tensor_tensor(minus_mean[:, one], moments[:, k, 0:1], norm_const[:, 2:3], ALU.mult)\
                        .then_inc(var_done[k], 1)
                pool.wait_ge(var_done[k], (1 if k == 1 else 2) * (t + 1))
                gp.tensor_tensor(rstd[:, one], var_eps[:, one], norm_const[:, 1:2], ALU.pow)\
                    .then_inc(rstd_done[k], 1)
                if k != 1:
                    pool.wait_ge(rstd_done[k], t + 1)
                    gp.tensor_tensor(offset[:, one], minus_mean[:, one], rstd[:, one], ALU.mult)\
                        .then_inc(offset_done[k], 1)

            def step(i, odd, n, a, b, c, d, e, f):
                looped = not isinstance(i, int)
                t0, t1, t2, t3, t4, t5 = i + 1, i - 1, i - 2, i - 3, i - 4, i - 5
                o1 = 1 - odd
                if f and a:
                    pool.wait_ge(scaled_done, t5 + 1)
                    pool.wait_ge(x2_biased_done, t5 + 1)
                    gp.tensor_tensor(xsum3[:, o1, :], xsum3[:, o1, :], x2_biased[:, o1, :], ALU.add)\
                        .then_inc(sum3_done, 1)
                if e and a:
                    pool.wait_ge(u_high_done, t4 + 1)
                    gp.tensor_tensor(u_low[:, :, :], u[:, :, :], u_high[:, :, :].bitcast(F32),
                                     ALU.subtract).then_inc(u_low_done, 1)
                if b:
                    pool.wait_ge(x_inv_done, t1 + 1)
                    if looped or t1 >= 1:
                        pool.wait_ge(diag_turned, 2 * t1)
                    for bb in range(2):
                        rows = slice(bb * T, (bb + 1) * T)
                        gp.tensor_tensor(xdiag[rows, :, bb * T:(bb + 1) * T], xprob[rows, :, :],
                                         x_inv[rows, :].unsqueeze(2).to_broadcast([T, XH, LH]), ALU.mult)\
                            .then_inc(x_normed, 1)
                        pool.wait_ge(x_normed, 2 * t1 + bb + 1)
                if n:
                    power(0, t0, x1_done)
                if f:
                    power(2, t5, x3_done)
                if not looped and i == 3:
                    pool.wait_ge(small_loaded, SMALL)
                if d:
                    pool.wait_ge(x2_done, t3 + 1)
                    if looped or t3 >= 2:
                        pool.wait_ge(sum3_done, t3 - 1)
                    gp.tensor_tensor(x2_biased[:, o1, :], x2[:, o1, :], fbias_row[:, :], ALU.add)\
                        .then_inc(x2_biased_done, 1)
                if c:
                    power(1, t2, x2_done)

            fixed_step(step, -1)
            fixed_step(step, 0)
            pool.wait_ge(scales_high, 1)
            rows = slice(PART, PART + E)
            gp.tensor_tensor(scales[rows, :, :], scales_raw[rows, :, :], scales[rows, :, :].bitcast(F32),
                             ALU.subtract).then_inc(scales_ready, 1)
            pool.wait_ge(scales_ready, 1)
            fixed_step(step, 1)
            over_tiles(pool, step)


def _shape_constants():
    freqs = (1.0 / np.float32(10000.0) ** (np.arange(0, D, 2, dtype=np.float32) / D)).astype(np.float32)
    angle = np.arange(T, dtype=np.float32)[None, :] * freqs[:, None]
    cos, sin = np.cos(angle).astype(np.float32), np.sin(angle).astype(np.float32)
    table = np.zeros((P, CONSTS), np.float32)
    table[:, COS:COS + T] = np.concatenate([cos, cos])
    table[:, SIN:SIN + T] = np.concatenate([-sin, sin])
    late = np.arange(T)[None, :] > (np.arange(P) % T)[:, None]
    table[:, MASK:MASK + T] = np.where(late, np.float32(MASKED), np.float32(0))
    table[:, IDENT:IDENT + P] = np.eye(P, dtype=np.float32)
    return table


def _halves(w, heads):
    return w.reshape(C, heads, D // 2, 2).transpose(0, 1, 3, 2).reshape(C, heads, D)


def kernel(**inputs):
    from concourse import bacc
    from concourse.bass_utils import run_bass_kernel_spmd

    a = {k: np.ascontiguousarray(v) for k, v in inputs.items()}
    wk = _halves(a["L0_attn_Wk"], G).reshape(C, G, 1, D)
    wq = _halves(a["L0_attn_Wq"], G * REP).reshape(C, G, REP, D)
    wv = a["L0_attn_Wv"].reshape(C, G, 1, D)
    wqkv = np.concatenate([wk, wq, wv], axis=2).reshape(KT, P, G, GCOLS).transpose(2, 1, 0, 3)
    wo = a["L0_attn_Wo"].reshape(G, REP, D, C).transpose(0, 2, 1, 3)
    arrays = {
        "x": a["x"].reshape(TOKENS, C), "ctx": a["ctx_4096"].reshape(TOKENS, C),
        "wqkv": wqkv, "wo": wo, "attn_bo": a["L0_attn_bo"], "consts": _shape_constants(),
        "x_wq": a["L0_xattn_Wq"].T, "x_bq": a["L0_xattn_bq"], "x_wk": a["L0_xattn_Wk"].T,
        "x_bk": a["L0_xattn_bk"], "x_wv": a["L0_xattn_Wv"].T, "x_bv": a["L0_xattn_bv"],
        "x_wo": a["L0_xattn_Wo"].T, "x_bo": a["L0_xattn_bo"], "f_w": a["L0_ffn_weight"].T,
        "f_bias": a["L0_ffn_bias"], "f_gate": a["L0_ffn_gate_w"].T,
        "f_in": a["L0_ffn_in_channel_scale"], "f_out": a["L0_ffn_out_channel_scale"],
    }
    arrays = {f"in_{k}": np.ascontiguousarray(v) for k, v in arrays.items()}
    nc = bacc.Bacc("TRN2", target_bir_lowering=False, num_devices=1)
    args = [nc.dram_tensor(k, v.shape, mybir.dt.from_np(v.dtype), kind="ExternalInput").ap()
            for k, v in arrays.items()]
    args.append(nc.dram_tensor("out", (TOKENS, C), F32, kind="ExternalOutput").ap())
    decoder_layer(nc, *args)
    result = run_bass_kernel_spmd(nc, [arrays], core_ids=[0])
    return result.results[0]["out"].reshape(B, T, C)
```
